# Optimizing a Trainium2 kernel written in Bass

```python
import numpy as np
import jax
import jax.numpy as jnp

def _softmax(x, axis=-1):
    return jax.nn.softmax(x, axis=axis)

def _gelu(x):
    return jax.nn.gelu(x, approximate=True)

def _silu(x):
    return jax.nn.silu(x)

def _sigmoid(x):
    return jax.nn.sigmoid(x)

def _layernorm(x, axis=-1, eps=1e-05):
    m = jnp.mean(x, axis=axis, keepdims=True)
    v = jnp.var(x, axis=axis, keepdims=True)
    return (x - m) / jnp.sqrt(v + eps)

def _scatter_add(tgt, idx, src, axis=0):
    return tgt.at[idx].add(src)

def _segment_sum(src, seg, n):
    return jax.ops.segment_sum(src, seg, n)
kernel_name = 'mk_early_fusion_embed_d1_tok_img768_r4_2223f8'

def setup_inputs(seed: int=0):
    np.random.seed(seed)
    _w = jnp.asarray

    def _rec_inputs():
        import jax
        import jax.numpy as jnp
        _rk = jax.random.key(seed)
        x = -0.000222058 + 0.999998 * jax.random.normal(jax.random.fold_in(_rk, 1), (32, 3, 84, 84), jnp.float32)
        x_txt = jax.random.randint(jax.random.fold_in(_rk, 51), (32, 128), 0, 12563, jnp.int32)
        return (x, x_txt)
    x, x_txt = _rec_inputs()

    def _L0_tok_setup():
        import jax, jax.numpy as jnp
        import numpy as np
        from jax import lax
        HIDDEN = 192
        C_IN = 3
        PATCH = 16
        SIDE = 32
        NUM_PATCHES = SIDE * SIDE

        def _position_ids(nb_h, nb_w):
            boundaries = np.arange(1.0 / SIDE, 1.0, 1.0 / SIDE, dtype=np.float32)
            frac_h = np.arange(0.0, 1.0 - 1e-06, 1.0 / nb_h, dtype=np.float32)
            frac_w = np.arange(0.0, 1.0 - 1e-06, 1.0 / nb_w, dtype=np.float32)
            bh = np.searchsorted(boundaries, frac_h, side='right')
            bw = np.searchsorted(boundaries, frac_w, side='right')
            return jnp.asarray((bh[:, None] * SIDE + bw).reshape(-1), dtype=jnp.int32)
        key = jax.random.key(seed)
        k1, k2, k3 = jax.random.split(key, 3)
        pixel_values = jax.random.normal(k1, (32, C_IN, 128, 128), dtype=jnp.float32)
        conv_w = jax.random.normal(k2, (HIDDEN, C_IN, PATCH, PATCH), dtype=jnp.float32) * 0.02
        conv_b = jnp.zeros((HIDDEN,), dtype=jnp.float32)
        pos_table = jax.random.normal(k3, (NUM_PATCHES, HIDDEN), dtype=jnp.float32) * 0.02
        return {'pixel_values': pixel_values, 'conv_w': conv_w, 'conv_b': conv_b, 'pos_table': pos_table}
    _L0_tok_all = _L0_tok_setup()
    _L0_tok_in = {k: v for k, v in _L0_tok_all.items() if k in ('conv_w', 'conv_b', 'pos_table')}
    del _L0_tok_all

    def _L0_txt_setup():
        import jax, jax.numpy as jnp
        import numpy as np
        VOCAB, N_TURNS, OUT_DIM, POLY_DEG, MAX_POS = (50257, 8, 192, 4, 512)
        B, S = (16, 512)
        LN_EPS = 1e-12
        key = jax.random.key(seed)
        k1, k2, k3, k4 = jax.random.split(key, 4)
        turns = jax.random.randint(k1, (VOCAB, N_TURNS), -10, 11).astype(jnp.float32)
        poly_coeffs = jax.random.normal(k2, (N_TURNS, POLY_DEG + 1, OUT_DIM), dtype=jnp.float32) * 0.02
        pos_table = jax.random.normal(k3, (MAX_POS, OUT_DIM), dtype=jnp.float32) * 0.02
        ln_gamma = jnp.ones((OUT_DIM,), dtype=jnp.float32)
        ln_beta = jnp.zeros((OUT_DIM,), dtype=jnp.float32)
        input_ids = jax.random.randint(k4, (B, S), 0, VOCAB)
        return {'turns': turns, 'poly_coeffs': poly_coeffs, 'pos_table': pos_table, 'ln_gamma': ln_gamma, 'ln_beta': ln_beta, 'input_ids': input_ids}
    _L0_txt_all = _L0_txt_setup()
    _L0_txt_in = {k: v for k, v in _L0_txt_all.items() if k in ('turns', 'poly_coeffs', 'pos_table', 'ln_gamma', 'ln_beta')}
    del _L0_txt_all

    def _L0_attn_setup():
        import jax, jax.numpy as jnp
        import numpy as np
        ALPHA = 0.35
        BITS_A = 8
        BITS_W = 8
        BITS_S = 4
        NUM_HEADS = 12

        def round_ln(x):
            y = jnp.floor(jnp.log2(x))
            up = x - 2.0 ** y > 2.0 ** (y + 1.0) - x
            return y + up.astype(x.dtype)

        def fq_act(x, bits=BITS_A):
            xmin = x.min()
            xmax = x.max()
            scale = jnp.maximum((xmax - xmin) / (2.0 ** bits - 1.0), 1e-08)
            zp = jnp.round(-xmin / scale)
            q = jnp.clip(jnp.round(x / scale) + zp, 0.0, 2.0 ** bits - 1.0)
            return ((q - zp) * scale, scale)

        def fq_weight(w, bits=BITS_W):
            wmax = jnp.maximum(jnp.abs(w).max(axis=1, keepdims=True), 1e-08)
            scale = wmax / (2.0 ** (bits - 1) - 1.0)
            q = jnp.clip(jnp.round(w / scale), -2.0 ** (bits - 1), 2.0 ** (bits - 1) - 1.0)
            return q * scale

        def _int_polynomial(x_int, sf):
            c0, c1, c2 = (0.35815147, 0.96963238, 1.0)
            b_int = jnp.floor(c1 / c0 / sf)
            c_int = jnp.floor(c2 / c0 / (sf * sf))
            z = x_int * (x_int + b_int) + c_int
            return (z, c0 * sf * sf)

        def _int_exp(x_int, sf):
            ln2 = -0.6931
            n = 30.0
            x0_int = jnp.floor(ln2 / sf)
            x_int = jnp.maximum(x_int, n * x0_int)
            qf = jnp.floor(x_int / x0_int)
            r = x_int - x0_int * qf
            exp_int, exp_sf = _int_polynomial(r, sf)
            exp_int = jnp.maximum(jnp.floor(exp_int * 2.0 ** (n - qf)), 0.0)
            return (exp_int, exp_sf / 2.0 ** n)

        def log_int_softmax(x, sf, bits=BITS_S):
            x_int = x / sf
            x_int = x_int - x_int.max(axis=-1, keepdims=True)
            exp_int, _ = _int_exp(x_int, sf)
            exp_sum = exp_int.sum(axis=-1, keepdims=True)
            BIG = 2.0 ** 31
            ratio = jnp.where(exp_int > 0.0, exp_sum / jnp.maximum(exp_int, 1.0), BIG)
            softmax_out = jnp.round(ratio)
            rounds = round_ln(jnp.maximum(softmax_out, 1.0))
            mask = rounds >= 2.0 ** bits
            qlog = jnp.clip(rounds, 0.0, 2.0 ** bits - 1.0)
            return jnp.where(mask, 0.0, 2.0 ** (-qlog))
        key = jax.random.key(seed)
        ks = jax.random.split(key, 5)
        B, N, C = (64, 197, 192)
        return {'x': jax.random.normal(ks[0], (B, N, C), jnp.float32), 'qkv_w': jax.random.normal(ks[1], (3 * C, C), jnp.float32) * 0.02, 'qkv_b': jax.random.normal(ks[2], (3 * C,), jnp.float32) * 0.02, 'proj_w': jax.random.normal(ks[3], (C, C), jnp.float32) * 0.02, 'proj_b': jax.random.normal(ks[4], (C,), jnp.float32) * 0.02}
    _L0_attn_all = _L0_attn_setup()
    _L0_attn_in = {k: v for k, v in _L0_attn_all.items() if k in ('qkv_w', 'qkv_b', 'proj_w', 'proj_b')}
    del _L0_attn_all

    def _L0_ffn_setup():
        import jax, jax.numpy as jnp
        import numpy as np
        B, T, H, F, E = (128, 32, 192, 768, 3)
        key = jax.random.key(seed)
        ks = jax.random.split(key, 4)
        s = 0.02
        return {'x': jax.random.normal(ks[0], (B, T, H), jnp.float32), 'Wg': jax.random.normal(ks[1], (E, H), jnp.float32) * s, 'W1': jax.random.normal(ks[2], (E, H, F), jnp.float32) * s, 'b1': jnp.zeros((E, F), jnp.float32), 'W2': jax.random.normal(ks[3], (E, F, H), jnp.float32) * s, 'b2': jnp.zeros((E, H), jnp.float32)}
    _L0_ffn_all = _L0_ffn_setup()
    _L0_ffn_in = {k: v for k, v in _L0_ffn_all.items() if k in ('Wg', 'W1', 'b1', 'W2', 'b2')}
    del _L0_ffn_all
    return {'x': x, 'x_txt': x_txt, 'L0_tok_conv_w': _L0_tok_in['conv_w'], 'L0_tok_conv_b': _L0_tok_in['conv_b'], 'L0_tok_pos_table': _L0_tok_in['pos_table'], 'L0_txt_turns': _L0_txt_in['turns'], 'L0_txt_poly_coeffs': _L0_txt_in['poly_coeffs'], 'L0_txt_pos_table': _L0_txt_in['pos_table'], 'L0_txt_ln_gamma': _L0_txt_in['ln_gamma'], 'L0_txt_ln_beta': _L0_txt_in['ln_beta'], 'L0_attn_qkv_w': _L0_attn_in['qkv_w'], 'L0_attn_qkv_b': _L0_attn_in['qkv_b'], 'L0_attn_proj_w': _L0_attn_in['proj_w'], 'L0_attn_proj_b': _L0_attn_in['proj_b'], 'L0_ffn_Wg': _L0_ffn_in['Wg'], 'L0_ffn_W1': _L0_ffn_in['W1'], 'L0_ffn_b1': _L0_ffn_in['b1'], 'L0_ffn_W2': _L0_ffn_in['W2'], 'L0_ffn_b2': _L0_ffn_in['b2']}

def reference(x, x_txt, L0_tok_conv_w, L0_tok_conv_b, L0_tok_pos_table, L0_txt_turns, L0_txt_poly_coeffs, L0_txt_pos_table, L0_txt_ln_gamma, L0_txt_ln_beta, L0_attn_qkv_w, L0_attn_qkv_b, L0_attn_proj_w, L0_attn_proj_b, L0_ffn_Wg, L0_ffn_W1, L0_ffn_b1, L0_ffn_W2, L0_ffn_b2):
    import jax
    import jax.numpy as jnp

    def _L0_tok_ref(pixel_values, conv_w, conv_b, pos_table):
        import jax, jax.numpy as jnp
        import numpy as np
        from jax import lax
        HIDDEN = 192
        C_IN = 3
        PATCH = 16
        SIDE = 32
        NUM_PATCHES = SIDE * SIDE

        def _position_ids(nb_h, nb_w):
            boundaries = np.arange(1.0 / SIDE, 1.0, 1.0 / SIDE, dtype=np.float32)
            frac_h = np.arange(0.0, 1.0 - 1e-06, 1.0 / nb_h, dtype=np.float32)
            frac_w = np.arange(0.0, 1.0 - 1e-06, 1.0 / nb_w, dtype=np.float32)
            bh = np.searchsorted(boundaries, frac_h, side='right')
            bw = np.searchsorted(boundaries, frac_w, side='right')
            return jnp.asarray((bh[:, None] * SIDE + bw).reshape(-1), dtype=jnp.int32)
        B, _, H, W = pixel_values.shape
        nb_h, nb_w = (H // PATCH, W // PATCH)
        patches = lax.conv_general_dilated(pixel_values, conv_w, window_strides=(PATCH, PATCH), padding='VALID', dimension_numbers=('NCHW', 'OIHW', 'NCHW'))
        patches = patches + conv_b[None, :, None, None]
        embeddings = patches.reshape(B, HIDDEN, nb_h * nb_w).transpose(0, 2, 1)
        pos_ids = _position_ids(nb_h, nb_w)
        pos_emb = pos_table[pos_ids]
        return embeddings + pos_emb[None, :, :]

    def _L0_txt_ref(turns, poly_coeffs, pos_table, ln_gamma, ln_beta, input_ids):
        import jax, jax.numpy as jnp
        import numpy as np
        VOCAB, N_TURNS, OUT_DIM, POLY_DEG, MAX_POS = (50257, 8, 192, 4, 512)
        B, S = (16, 512)
        LN_EPS = 1e-12
        b, s = input_ids.shape
        x = turns[input_ids]
        powers = x[..., None] ** jnp.arange(POLY_DEG + 1, dtype=x.dtype)
        emb = jnp.einsum('bstp,tpd->bsd', powers, poly_coeffs)
        emb = emb + pos_table[:s][None, :, :]
        mu = jnp.mean(emb, axis=-1, keepdims=True)
        var = jnp.mean(jnp.square(emb - mu), axis=-1, keepdims=True)
        out = (emb - mu) * jax.lax.rsqrt(var + LN_EPS) * ln_gamma + ln_beta
        return out

    def _L0_attn_ref(x, qkv_w, qkv_b, proj_w, proj_b):
        import jax, jax.numpy as jnp
        import numpy as np
        ALPHA = 0.35
        BITS_A = 8
        BITS_W = 8
        BITS_S = 4
        NUM_HEADS = 12

        def round_ln(x):
            y = jnp.floor(jnp.log2(x))
            up = x - 2.0 ** y > 2.0 ** (y + 1.0) - x
            return y + up.astype(x.dtype)

        def fq_act(x, bits=BITS_A):
            xmin = x.min()
            xmax = x.max()
            scale = jnp.maximum((xmax - xmin) / (2.0 ** bits - 1.0), 1e-08)
            zp = jnp.round(-xmin / scale)
            q = jnp.clip(jnp.round(x / scale) + zp, 0.0, 2.0 ** bits - 1.0)
            return ((q - zp) * scale, scale)

        def fq_weight(w, bits=BITS_W):
            wmax = jnp.maximum(jnp.abs(w).max(axis=1, keepdims=True), 1e-08)
            scale = wmax / (2.0 ** (bits - 1) - 1.0)
            q = jnp.clip(jnp.round(w / scale), -2.0 ** (bits - 1), 2.0 ** (bits - 1) - 1.0)
            return q * scale

        def _int_polynomial(x_int, sf):
            c0, c1, c2 = (0.35815147, 0.96963238, 1.0)
            b_int = jnp.floor(c1 / c0 / sf)
            c_int = jnp.floor(c2 / c0 / (sf * sf))
            z = x_int * (x_int + b_int) + c_int
            return (z, c0 * sf * sf)

        def _int_exp(x_int, sf):
            ln2 = -0.6931
            n = 30.0
            x0_int = jnp.floor(ln2 / sf)
            x_int = jnp.maximum(x_int, n * x0_int)
            qf = jnp.floor(x_int / x0_int)
            r = x_int - x0_int * qf
            exp_int, exp_sf = _int_polynomial(r, sf)
            exp_int = jnp.maximum(jnp.floor(exp_int * 2.0 ** (n - qf)), 0.0)
            return (exp_int, exp_sf / 2.0 ** n)

        def log_int_softmax(x, sf, bits=BITS_S):
            x_int = x / sf
            x_int = x_int - x_int.max(axis=-1, keepdims=True)
            exp_int, _ = _int_exp(x_int, sf)
            exp_sum = exp_int.sum(axis=-1, keepdims=True)
            BIG = 2.0 ** 31
            ratio = jnp.where(exp_int > 0.0, exp_sum / jnp.maximum(exp_int, 1.0), BIG)
            softmax_out = jnp.round(ratio)
            rounds = round_ln(jnp.maximum(softmax_out, 1.0))
            mask = rounds >= 2.0 ** bits
            qlog = jnp.clip(rounds, 0.0, 2.0 ** bits - 1.0)
            return jnp.where(mask, 0.0, 2.0 ** (-qlog))
        B, N, C = x.shape
        H = NUM_HEADS
        hd = C // H
        attn_scale = hd ** (-0.5)
        gmax = jnp.maximum(jnp.abs(x).max(axis=(0, 1)), 1e-08)
        wmax = jnp.maximum(jnp.abs(qkv_w).max(axis=0), 1e-08)
        cs = gmax ** ALPHA / wmax ** (1.0 - ALPHA)
        cs = 2.0 ** round_ln(cs)
        x_s = x / cs[None, None, :]
        w_s = qkv_w * cs[None, :]
        xq, _ = fq_act(x_s)
        wq = fq_weight(w_s)
        h = jnp.einsum('bnc,mc->bnm', xq, wq) + qkv_b
        h, _ = fq_act(h)
        qkv = h.reshape(B, N, 3, H, hd).transpose(2, 0, 3, 1, 4)
        q, k, v = (qkv[0], qkv[1], qkv[2])
        attn = jnp.einsum('bhnd,bhmd->bhnm', q, k) * attn_scale
        attn, a_scale = fq_act(attn)
        attn = log_int_softmax(attn, a_scale)
        out = jnp.einsum('bhnm,bhmd->bhnd', attn, v)
        out = out.transpose(0, 2, 1, 3).reshape(B, N, C)
        out, _ = fq_act(out)
        pw = fq_weight(proj_w)
        out = jnp.einsum('bnc,mc->bnm', out, pw) + proj_b
        out, _ = fq_act(out)
        return out

    def _L0_ffn_ref(x, Wg, W1, b1, W2, b2):
        import jax, jax.numpy as jnp
        import numpy as np
        B, T, H, F, E = (128, 32, 192, 768, 3)
        scores = jax.nn.softmax(jnp.mean(x, axis=1) @ Wg.T, axis=-1)
        _, idx = jax.lax.top_k(scores, 1)
        sel = idx[:, 0]
        h = jax.nn.gelu(jnp.einsum('bth,ehf->betf', x, W1) + b1[None, :, None, :], approximate=False)
        y = jnp.einsum('betf,efh->beth', h, W2) + b2[None, :, None, :]
        w = scores * jax.nn.one_hot(sel, E, dtype=scores.dtype)
        out = jnp.einsum('beth,be->bth', y, w)
        return out
    h = _L0_tok_ref(x, L0_tok_conv_w, L0_tok_conv_b, L0_tok_pos_table)
    h = jnp.concatenate([h, _L0_txt_ref(L0_txt_turns, L0_txt_poly_coeffs, L0_txt_pos_table, L0_txt_ln_gamma, L0_txt_ln_beta, x_txt)], axis=1)
    h = h + _L0_attn_ref(_layernorm(h, axis=-1), L0_attn_qkv_w, L0_attn_qkv_b, L0_attn_proj_w, L0_attn_proj_b)
    h = h + _L0_ffn_ref(_layernorm(h, axis=-1), L0_ffn_Wg, L0_ffn_W1, L0_ffn_b1, L0_ffn_W2, L0_ffn_b2)
    return h

_drawn_inputs = setup_inputs


def setup_inputs(seed=0):
    import zlib

    import numpy as np

    out = dict(_drawn_inputs(seed))
    spreads = {'L0_tok_conv_b': (0.0, 0.1),
     'L0_txt_ln_gamma': (1.0, 0.2),
     'L0_txt_ln_beta': (0.0, 0.1),
     'L0_ffn_b1': (0.0, 0.666),
     'L0_ffn_b2': (0.0, 0.1)}
    factors = {'L0_tok_pos_table': 6.754,
     'L0_txt_pos_table': 200.0,
     'L0_attn_qkv_b': 8.0,
     'L0_attn_proj_b': 2.85,
     'L0_ffn_Wg': 200.0}
    for name, (base, spread) in spreads.items():
        noise = np.random.default_rng([zlib.crc32(name.encode()), seed]).standard_normal(out[name].shape)
        drawn = base * np.exp(spread * noise) if base else spread * noise
        out[name] = jnp.asarray(drawn.astype(out[name].dtype))
    for name, factor in factors.items():
        out[name] = (out[name] * factor).astype(out[name].dtype)
    return out
```

```python
from contextlib import ExitStack

import numpy as np

import concourse.bass as bass
from concourse import mybir

ALU = mybir.AluOpType
ACT = mybir.ActivationFunctionType
F32 = mybir.dt.float32
BF16 = mybir.dt.bfloat16
I16 = mybir.dt.int16
I32 = mybir.dt.int32
AX = mybir.AxisListType.X
RMAX = bass.bass_isa.ReduceOp.max

P = 128
B, NI, NT = 32, 25, 128
N = NI + NT
T = B * N
IW = N - 32
ID = 32 - NI
C = 192
CK = (128, 64)
G = B // 4
NTILE = B + G
H, HD = 12, 16
HT = H // 4
RT = H + HT
E, FF = 3, 768
KI = 6
FT = FF // P
BIG = 3.0e38
LEVELS = 255.0
ROUND = 12582912.0
EXPONENT = -8388608


def ds(start, size):
    return bass.ds(start, size)


class Ctx:

    def __init__(self, nc, stack, dram):
        self.nc, self.stack, self.d = nc, stack, dram

    def sb(self, name, shape, dt=F32, stack=None):
        return (stack or self.stack).enter_context(self.nc.sbuf_tensor(name, shape, dt))

    def ps(self, name, shape, dt=F32, stack=None):
        return (stack or self.stack).enter_context(self.nc.psum_tensor(name, shape, dt))

    def sem(self, name):
        return self.stack.enter_context(self.nc.semaphore(name))


def embed(k, m):
    nc, d = k.nc, k.d
    Hres, xnT, ident = m["H"], m["xnT"], m["ident"]
    with ExitStack() as st:
        sb = lambda n, s, t=F32: k.sb(n, s, t, st)
        patches, wimg = sb("patches", [P, KI, G * P]), sb("wimg", [P, KI, C])
        posimg, convb, postxt = sb("posimg", [P, C]), sb("convb", [P, C]), sb("postxt", [P, C])
        gamma, beta, coef = sb("gamma", [P, C]), sb("beta", [P, C]), sb("coef", [P, C])
        ids, feat = sb("ids", [P, B], I32), sb("feat", [P, B, 64])
        raw = sb("raw", [P, B, 8])
        featT = sb("featT", [P, 4, P])
        stat = sb("stat", [P, 4, 6])
        mv4 = sb("mv4", [P, 4, 2])
        mv, rstd, root, newt = sb("mv", [P, NTILE, 2]), sb("rstd", [P, NTILE]), sb("root", [P, NTILE]), sb("newt", [P, NTILE])
        xn = sb("xn", [P, 2, 4, C])
        pimg, ptr = k.ps("pimg", [P, 2, 512], F32, st), k.ps("ptr", [P, 2, 512], F32, st)
        pemb = k.ps("pemb", [P, 2, 512], F32, st)

        in_img, in_small, in_ids = k.sem("in_img"), k.sem("in_small"), k.sem("in_ids")
        gathered = [k.sem(f"gathered{i}") for i in range(4)]
        iden = k.sem("iden")
        img_acc, img_out = k.sem("img_acc"), k.sem("img_out")
        pows, featT_ps, featT_sb, emb_acc, emb_out = (k.sem(x) for x in ("pows", "featT_ps", "featT_sb", "emb_acc", "emb_out"))
        lnv, lnroot, lnroot2, lnv2 = (k.sem(x) for x in ("lnv", "lnroot", "lnroot2", "lnv2"))
        st1, st2 = ([k.sem(f"{x}{y}") for y in ("stats", "aggr", "kept", "passed")] for x in "ab")
        xn_free, xn_done, xt_ps, xt_out = (k.sem(x) for x in ("xn_free", "xn_done", "xt_ps", "xt_out"))
        with nc.Block() as block:
            @block.sync
            def _(sp):
                sp.dma_start(ids[:, :], d["ids"]).then_inc(in_ids, 16)
                sp.dma_start(wimg[:, :, :], d["wimg"]).then_inc(in_img, 16)
                sp.dma_start(patches[:, :, :], d["patches"]).then_inc(in_img, 16)
                for t, n in ((posimg, "posimg"), (convb, "convb"), (postxt, "postxt"), (gamma, "gamma"), (beta, "beta"), (coef, "coef")):
                    sp.dma_start(t[:, :], d[n]).then_inc(in_small, 16)

            @block.gpsimd
            def _(pool):
                pool.memset(ident[:, :], 0.0).then_inc(iden, 1)
                pool.wait_ge(iden, 1)
                pool.affine_select(out=ident[:, :], in_=ident[:, :], compare_op=ALU.not_equal, fill=1.0,
                                   base=0, pattern=[[-1, P]], channel_multiplier=1).then_inc(iden, 1)
                pool.wait_ge(in_ids, 16)
                for b in range(B):
                    pool.indirect_dma_start(out=raw[:, b, :], out_offset=None, in_=d["turns"],
                                            in_offset=bass.IndirectOffsetOnAxis(ap=ids[:, b:b + 1], axis=0)
                                            ).then_inc(gathered[b // 8], 16)

            @block.tensor
            def _(pe):
                pe.sem_inc(featT_ps, 1)
                pe.sem_inc(xt_ps, 2)
                pe.wait_ge(in_img, 32)
                for g in range(G):
                    if g >= 2:
                        pe.wait_ge(img_out, g - 1)
                    for kt in range(KI):
                        mm = pe.matmul(pimg[:, g % 2, 0:C], patches[:, kt, ds(g * P, P)], wimg[:, kt, :],
                                       start=(kt == 0), stop=(kt == KI - 1))
                    mm.then_inc(img_acc, 1)
                pe.wait_ge(iden, 2)
                pe.wait_ge(in_small, 96)
                with pe.Fori(0, G) as g:
                    for u in range(2):
                        pe.wait_ge(pows, g * 2 + u + 1)
                        pe.wait_ge(featT_sb, g * 2 + u + 1)
                        pe.transpose(ptr[:, u, 0:P], featT[:, 2 + u, :], ident[:, :]).then_inc(featT_ps, 1)
                        pe.wait_ge(featT_sb, g * 2 + u + 2)
                        pe.wait_ge(emb_out, g * 2 + u + 1)
                        for v in range(2):
                            mm = pe.matmul(pemb[:, v, 0:C], featT[64 * v:64 * v + 64, u, :],
                                           coef[64 * v:64 * v + 64, :], start=True, stop=True)
                        mm.then_inc(emb_acc, 1)
                with pe.Fori(0, G) as g:
                    pe.wait_ge(xn_done, g * 2 + 1)
                    pe.wait_ge(xt_out, g * 4 + 4)
                    for kt in range(2):
                        for v in range(4):
                            mm = pe.transpose(ptr[0:CK[kt], kt, ds(v * P, P)], xn[:, 0, v, kt * P:kt * P + CK[kt]], ident[:, :])
                    mm.then_inc(xt_ps, 1)
                    pe.wait_ge(xn_done, g * 2 + 2)
                    for kt in range(2):
                        mm = pe.transpose(pemb[0:CK[kt], kt, 0:P], xn[:, 1, 0, kt * P:kt * P + CK[kt]], ident[:, :])
                    mm.then_inc(xt_ps, 1)

            @block.scalar
            def _(act):
                act.sem_inc(featT_sb, 1)
                act.sem_inc(xt_out, 4)
                with act.Fori(0, G) as g:
                    for u in range(2):
                        act.wait_ge(featT_ps, g * 2 + u + 2)
                        act.activation(featT[:, u, :], ptr[:, u, 0:P], ACT.Copy).then_inc(featT_sb, 1)
                act.wait_ge(lnv, 1)
                act.activation(root[:, 0:B], mv[:, 0:B, 1], ACT.Sqrt).then_inc(lnroot, 1)
                act.wait_ge(lnv2, 1)
                act.activation(root[:, :], mv[:, :, 1], ACT.Sqrt).then_inc(lnroot2, 1)
                with act.Fori(0, G) as g:
                    act.wait_ge(xt_ps, g * 2 + 3)
                    for kt in range(2):
                        act.activation(
                            xnT[0:CK[kt], kt, ds(g * 4 * N, 4 * N)].rearrange("p (v n) -> p v n", n=N)[:, :, 0:NT],
                            ptr[0:CK[kt], kt, :].rearrange("p (v n) -> p v n", n=P), ACT.Copy).then_inc(xt_out, 1)
                    act.wait_ge(xt_ps, g * 2 + 4)
                    for kt in range(2):
                        act.activation(
                            xnT[0:CK[kt], kt, ds(g * 4 * N, 4 * N)].rearrange("p (v n) -> p v n", n=N)[:, :, NT:N],
                            pemb[0:CK[kt], kt, 0:P].rearrange("p (v n) -> p v n", n=32)[:, :, ID:32], ACT.Copy).then_inc(xt_out, 1)

            @block.vector
            def _(v):
                link = chained(v, k.sem("embed_chain"))
                link(v.memset(feat[:, :, :], 0.0))
                link(v.memset(feat[:, :, 0:8], 1.0))
                v.wait_ge(in_small, 96)
                link(v.tensor_tensor(convb[:, :], convb[:, :], posimg[:, :], ALU.add))
                for g in range(G):
                    v.wait_ge(img_acc, g + 1)
                    v.tensor_tensor(Hres[:, B + g, :], pimg[:, g % 2, 0:C], convb[:, :], ALU.add).then_inc(img_out, 1)
                for i in range(4):
                    v.wait_ge(gathered[i], 128)
                r, f = raw[:, :, :], lambda p: feat[:, :, 8 * p:8 * p + 8]
                link(v.tensor_copy(f(1), r))
                link(v.tensor_tensor(f(2), r, r, ALU.mult))
                v.tensor_tensor(f(3), f(2), r, ALU.mult)
                link(v.tensor_tensor(f(4), f(2), f(2), ALU.mult))
                pos2 = postxt[:, :].unsqueeze(1).to_broadcast([P, 2, C])
                v.wait_ge(iden, 2)
                v.sem_inc(emb_out, 1)
                with v.Fori(0, G) as g:
                    for u in range(2):
                        v.wait_ge(featT_ps, g * 2 + u + 1)
                        v.tensor_copy(featT[:, 2 + u, :], feat[:, ds(g * 4 + 2 * u, 2), :].rearrange("p b f -> p (b f)")).then_inc(pows, 1)
                        v.wait_ge(emb_acc, g * 2 + u + 1)
                        v.tensor_tensor(Hres[:, ds(g * 4 + 2 * u, 2), :], pemb[:, :, 0:C], pos2, ALU.add).then_inc(emb_out, 1)
                v.wait_ge(emb_out, B // 2 + 1)
                norm_stats(v, Hres, stat, mv4, mv, B // 4, st1)

                def rsqrt(n, e, ready, rooted):
                    v.tensor_scalar(mv[:, 0:n, 1], mv[:, 0:n, 1], e, None, ALU.add).then_inc(ready, 1)
                    v.wait_ge(rooted, 1)
                    newton(v, link, mv[:, 0:n, 1], root[:, 0:n], newt[:, 0:n], rstd[:, 0:n])

                rsqrt(B, 1e-12, lnv, lnroot)
                gb = gamma[:, :].unsqueeze(1).to_broadcast([P, 4, C])
                bb = beta[:, :].unsqueeze(1).to_broadcast([P, 4, C])
                ln_a, ln_b = k.sem("ln_a"), k.sem("ln_b")
                with v.Fori(0, G) as g:
                    for w in range(4):
                        v.tensor_scalar(Hres[:, g * 4 + w, :], Hres[:, g * 4 + w, :], mv[:, g * 4 + w, 0:1],
                                        rstd[:, ds(g * 4 + w, 1)], ALU.subtract, ALU.mult).then_inc(ln_a, 1)
                    h4 = Hres[:, ds(g * 4, 4), :]
                    v.wait_ge(ln_a, g * 4 + 4)
                    v.tensor_tensor(h4, h4, gb, ALU.mult).then_inc(ln_b, 1)
                    v.wait_ge(ln_b, g * 2 + 1)
                    v.tensor_tensor(h4, h4, bb, ALU.add).then_inc(ln_b, 1)
                v.wait_ge(ln_b, 2 * G)
                norm_stats(v, Hres, stat, mv4, mv, NTILE // 4, st2)
                rsqrt(NTILE, 1e-5, lnv2, lnroot2)
                with v.Fori(0, G) as g:
                    v.wait_ge(xt_ps, g * 2 + 2)
                    for w in range(4):
                        ins = v.tensor_scalar(xn[:, 0, w, :], Hres[:, g * 4 + w, :], mv[:, g * 4 + w, 0:1],
                                              rstd[:, ds(g * 4 + w, 1)], ALU.subtract, ALU.mult)
                    ins.then_inc(xn_done, 1)
                    v.tensor_scalar(xn[:, 1, 0, :], Hres[:, g + B, :], mv[:, g + B, 0:1],
                                    rstd[:, ds(g + B, 1)], ALU.subtract, ALU.mult).then_inc(xn_done, 1)


def wait_apart(eng, sem, value, passed):
    eng.wait_ge(sem, value)
    eng.sem_inc(passed, 1)


def chained(eng, sem):
    seq = [0]

    def link(ins):
        seq[0] += 1
        ins.then_inc(sem, 1)
        eng.wait_ge(sem, seq[0])
    return link


def quant_params(v, link, mm, q):
    link(v.tensor_tensor(q[:, 0:1], mm[:, 0:1], mm[:, 1:2], ALU.add))
    link(v.tensor_scalar(q[:, 0:1], q[:, 0:1], 1.0 / LEVELS, 1e-8, ALU.mult, ALU.max))
    link(v.reciprocal(q[:, 1:2], q[:, 0:1]))
    link(v.tensor_tensor(q[:, 2:3], mm[:, 1:2], q[:, 1:2], ALU.mult))
    link(v.tensor_scalar(q[:, 2:3], q[:, 2:3], ROUND, ROUND, ALU.add, ALU.subtract))
    link(v.tensor_scalar(q[:, 3:4], q[:, 2:3], -1.0, LEVELS, ALU.mult, ALU.add))


def quant_inputs(k, m):
    nc, d = k.nc, k.d
    xnT, ident, xqT, wqT = m["xnT"], m["ident"], m["xqT"], m["wqT"]
    with ExitStack() as st:
        sb = lambda n, s, t=F32: k.sb(n, s, t, st)
        wc, wp, wd = sb("wc", [P, 2, 3 * C]), sb("wp", [P, 9, C]), sb("wd", [P, 5, C])
        ext, wmax, cs, rcs = sb("ext", [P, 2, 2]), sb("wmax", [P, 2]), sb("cs", [P, 2]), sb("rcs", [P, 2])
        lng, lnw = sb("lng", [P, 2]), sb("lnw", [P, 2])
        mm1, mm2 = sb("mm1", [P, 2]), sb("mm2", [P, 2])
        qx, inv = m["qx"], sb("inv", [P, 2])
        ones, diag, csrow = sb("ones", [P, P]), sb("diag", [P, 2, P]), sb("csrow", [P, C])
        wp16, wpb = sb("wp16", [P, 9, C], I16), sb("wpb", [P, 9, 2 * P], BF16)
        xi = sb("xi", [P, 2, T], I16)
        identb = m["identb"]
        pcs, pw = k.ps("pcs", [P, 512], F32, st), k.ps("pw", [P, 2, 1024], BF16, st)
        in_w, chmm, lns, cs_raw, csd, csps, xr, xred, wready, wps, wcp, chain = (
            k.sem(x) for x in ("in_w", "chmm", "lns", "cs_raw", "csd", "csps", "xr", "xred", "wready", "wps", "wcp", "scale_chain"))
        with nc.Block() as block:
            @block.sync
            def _(sp):
                for t, n in ((wc, "wc"), (wp, "wp"), (wd, "wd")):
                    sp.dma_start(t[:, :, :], d[n]).then_inc(in_w, 16)
                sp.dma_start(m["biasp"][:, :], d["biasp"]).then_inc(in_w, 16)
                sp.dma_start(m["biasd"][:, :], d["biasd"]).then_inc(in_w, 16)
                sp.wait_ge(in_w, 80)

            @block.gpsimd
            def _(pool):
                pool.wait_ge(xr, 1)
                pool.partition_all_reduce(mm2[:, :], mm1[:, :], P, RMAX).then_inc(xred, 1)

            @block.scalar
            def _(act):
                act.wait_ge(chmm, 1)
                act.activation(lng[:, :], cs[:, :], ACT.Ln).then_inc(lns, 1)
                act.activation(lnw[:, :], wmax[:, :], ACT.Ln).then_inc(lns, 1)
                act.wait_ge(cs_raw, 1)
                act.activation(cs[:, :], lng[:, :], ACT.Exp).then_inc(lns, 1)

            @block.tensor
            def _(pe):
                pe.wait_ge(csd, 1)
                for kt in range(2):
                    mm = pe.matmul(pcs[:, kt * P:kt * P + CK[kt]], ones[:, :], diag[:, kt, 0:CK[kt]], start=True, stop=True)
                mm.then_inc(csps, 1)
                pe.wait_ge(wready, 1)
                for kt in range(2):
                    pe.wait_ge(wready, 1)
                    for t in range(8):
                        mm = pe.transpose(pw[:, kt, t * P:(t + 1) * P], wpb[:, t, kt * P:kt * P + P], identb[:, :])
                    mm.then_inc(wps, 1)
                pe.wait_ge(wcp, 2)
                for kt in range(2):
                    mm = pe.transpose(pw[:, kt, 0:P], wpb[:, 8, kt * P:kt * P + P], identb[:, :])
                mm.then_inc(wps, 1)

            @block.vector
            def _(v):
                link = chained(v, chain)
                link(v.memset(ones[:, :], 1.0))
                link(v.tensor_copy(identb[:, :], ident[:, :]))
                link(v.memset(wpb[:, :, C:2 * P], 0.0))
                link(v.memset(ext[:, :, :], 0.0))
                link(v.memset(xqT[:, 1, :], 0.0))
                for kt in range(2):
                    c = CK[kt]
                    link(v.tensor_reduce(ext[0:c, 0, kt:kt + 1], xnT[0:c, kt, :], AX, ALU.max))
                    link(v.tensor_reduce(ext[0:c, 1, kt:kt + 1], xnT[0:c, kt, :], AX, ALU.min, negate=True))
                link(v.tensor_tensor(cs[:, :], ext[:, 0, :], ext[:, 1, :], ALU.max))
                link(v.tensor_scalar(cs[:, :], cs[:, :], 1e-8, None, ALU.max))
                v.wait_ge(in_w, 80)
                link(v.tensor_reduce(wmax[:, :], wc[:, :, :], AX, ALU.max, apply_absolute_value=True))
                v.tensor_scalar(wmax[:, :], wmax[:, :], 1e-8, None, ALU.max).then_inc(chmm, 1)
                v.wait_ge(lns, 2)
                link(v.tensor_scalar(lng[:, :], lng[:, :], 0.35, None, ALU.mult))
                link(v.tensor_scalar(lnw[:, :], lnw[:, :], 0.65, None, ALU.mult))
                v.tensor_tensor(lng[:, :], lng[:, :], lnw[:, :], ALU.subtract).then_inc(cs_raw, 1)
                v.wait_ge(lns, 3)
                link(v.tensor_scalar(cs[:, :], cs[:, :], 4.0 / 3.0, None, ALU.mult))
                link(v.tensor_scalar(cs[:, :].bitcast(I32), cs[:, :].bitcast(I32), EXPONENT, None, ALU.bitwise_and))
                link(v.reciprocal(rcs[:, :], cs[:, :]))
                for kt in range(2):
                    ins = v.tensor_scalar(diag[:, kt, :], ident[:, :], cs[:, kt:kt + 1], None, ALU.mult)
                ins.then_inc(csd, 1)
                rc2 = rcs[:, :].unsqueeze(1).to_broadcast([P, 2, 2])
                link(v.tensor_tensor(ext[:, :, :], ext[:, :, :], rc2, ALU.mult))
                v.tensor_reduce(mm1[:, :], ext[:, :, :], AX, ALU.max).then_inc(xr, 1)
                v.wait_ge(csps, 1)
                link(v.tensor_copy(csrow[:, :], pcs[:, 0:C]))
                link(v.tensor_tensor(wp[:, :, :], wp[:, :, :], csrow[:, :].unsqueeze(1).to_broadcast([P, 9, C]), ALU.mult))
                link(v.tensor_tensor(wd[:, :, :], wd[:, :, :], csrow[:, :].unsqueeze(1).to_broadcast([P, 5, C]), ALU.mult))
                sp9, sd5 = m["ap"], m["ad"]
                for rows, s in ((wp, sp9), (wd, sd5)):
                    link(v.tensor_reduce(s[:, :], rows[:, :, :], AX, ALU.max, apply_absolute_value=True))
                    link(v.tensor_scalar(s[:, :], s[:, :], 1e-8, 1.0 / 127.0, ALU.max, ALU.mult))
                winv = sb("winv", [P, 9])
                link(v.reciprocal(winv[:, :], sp9[:, :]))
                link(v.tensor_tensor(wp16[:, :, :], wp[:, :, :], winv[:, :].unsqueeze(2).to_broadcast([P, 9, C]), ALU.mult))
                link(v.tensor_scalar(wpb[:, :, 0:C], wp16[:, :, :], -128.0, 127.0, ALU.max, ALU.min))
                v.tensor_copy(wpb[:, :, 0:C], wpb[:, :, 0:C]).then_inc(wready, 1)
                v.wait_ge(xred, 1)
                quant_params(v, link, mm2, qx)
                link(v.tensor_scalar(inv[:, :], rcs[:, :], qx[:, 1:2], None, ALU.mult))
                for kt in range(2):
                    c = CK[kt]
                    link(v.tensor_scalar(xi[0:c, kt, :], xnT[0:c, kt, :], inv[0:c, kt:kt + 1], qx[0:c, 3:4], ALU.mult, ALU.min))
                    link(v.tensor_copy(xqT[0:c, kt, :], xi[0:c, kt, :]))
                for kt in range(2):
                    v.wait_ge(wps, kt + 1)
                    v.tensor_copy(wqT[:, kt, 0:8 * P], pw[:, kt, :]).then_inc(wcp, 1)
                v.wait_ge(wps, 3)
                link(v.tensor_copy(wqT[:, :, 8 * P:9 * P], pw[:, :, 0:P]))
                v.wait_ge(wcp, 2)
                for kt in range(2):
                    link(v.tensor_copy(m["wdT"][:, kt, 0:4 * P], heads16(wqT, kt, 0, 32)))
                    link(v.tensor_copy(m["wdT"][:, kt, 4 * P:5 * P], heads16(wqT, kt, 28, 8)))
                    link(v.tensor_copy(m["xqI"][:, kt, :], image_cols(xqT[:, kt, :])))
                link(v.tensor_scalar(sp9[:, :], sp9[:, :], qx[:, 0:1], None, ALU.mult))
                link(v.tensor_scalar(sd5[:, :], sd5[:, :], qx[:, 0:1], None, ALU.mult))


def heads16(w, kt, first, count):
    return w[:, kt, first * 32:(first + count) * 32].rearrange("p (h f) -> p h f", f=32)[:, :, 0:HD]


def image_cols(x):
    return x.rearrange("p (b n) -> p b n", n=N)[:, :, IW:N]


def range_h(k, m):
    nc = k.nc
    xqT, wqT = m["xqT"], m["wqT"]
    NCH, W = 24, T // 24
    with ExitStack() as st:
        sb = lambda n, s, t=F32: k.sb(n, s, t, st)
        top, low = sb("top", [P, 5, NCH]), sb("low", [P, 5, NCH])
        hm, mm1, mm2 = sb("hm", [P, 2, 5]), sb("hm1", [P, 2]), sb("hm2", [P, 2])
        ph = k.ps("ph", [P, 2, 6, 256], F32, st)
        prod, seen, hr, hred, chain = (k.sem(x) for x in ("h_prod", "h_seen", "hr", "hred", "h_chain"))
        with nc.Block() as block:
            @block.tensor
            def _(pe):
                with pe.Fori(0, NCH // 2) as i:
                    for u in range(2):
                        pe.wait_ge(seen, i * 4 + 2 * u + 2)
                        for t in range(5):
                            for kt in range(2):
                                mm = pe.matmul(ph[:, u, t, 0:W], m["wdT"][:, kt, t * P:(t + 1) * P],
                                               xqT[:, kt, ds(i * (2 * W) + u * W, W)], start=(kt == 0), stop=(kt == 1))
                        mm.then_inc(prod, 1)

            @block.gpsimd
            def _(pool):
                pool.wait_ge(hr, 1)
                pool.partition_all_reduce(mm2[:, :], mm1[:, :], P, RMAX).then_inc(hred, 1)

            @block.vector
            def _(v):
                link = chained(v, chain)
                v.sem_inc(seen, 4)
                with v.Fori(0, NCH // 2) as i:
                    for u in range(2):
                        v.wait_ge(prod, i * 2 + u + 1)
                        v.tensor_reduce(top[:, :, ds(i * 2 + u, 1)], ph[:, u, 0:5, 0:W], AX, ALU.max).then_inc(seen, 1)
                        v.tensor_reduce(low[:, :, ds(i * 2 + u, 1)], ph[:, u, 0:5, 0:W], AX, ALU.min).then_inc(seen, 1)
                v.wait_ge(seen, 4 + 2 * NCH)
                link(v.tensor_reduce(hm[:, 0, :], top[:, :, :], AX, ALU.max))
                link(v.tensor_reduce(hm[:, 1, :], low[:, :, :], AX, ALU.min))
                link(v.tensor_tensor(hm[:, :, :], hm[:, :, :], m["ad"][:, :].unsqueeze(1).to_broadcast([P, 2, 5]), ALU.mult))
                link(v.tensor_tensor(hm[:, :, :], hm[:, :, :], m["biasd"][:, :].unsqueeze(1).to_broadcast([P, 2, 5]), ALU.add))
                link(v.tensor_reduce(mm1[:, 0:1], hm[:, 0, :], AX, ALU.max))
                v.tensor_reduce(mm1[:, 1:2], hm[:, 1, :], AX, ALU.min, negate=True).then_inc(hr, 1)
                v.wait_ge(hred, 1)
                quant_params(v, link, mm2, m["qh"])
                link(v.tensor_scalar(m["ap"][:, :], m["ap"][:, :], m["qh"][:, 1:2], None, ALU.mult))
                link(v.tensor_scalar(m["biasp"][:, :], m["biasp"][:, :], m["qh"][:, 1:2], None, ALU.mult))


def quant_qkv(k, m):
    nc, d = k.nc, k.d
    xqT, xqI, wqT, qk, vt, vi = (m[x] for x in ("xqT", "xqI", "wqT", "qk", "vt", "vi"))
    NCH, W = B // 2, 2 * N
    with ExitStack() as st:
        sb = lambda n, s, t=F32: k.sb(n, s, t, st)
        qi = sb("qi", [P, 2, 3, W], I16)
        ones, diag, rows, ident = sb("ones_v", [P, P]), sb("diag_v", [P, 2, 3, P]), sb("rows_v", [P, 2, C]), m["ident"]
        vf, v16 = sb("vf", [P, 2, 2, C]), sb("v16", [P, 2, 2, C], I16)
        pq, pv = k.ps("pq", [P, 2, 3, 512], F32, st), k.ps("pv", [P, 2, 512], F32, st)
        q_prod, q_int, q_done, diag_ok, row_ps, v_prod, v_scaled, v_int, v_done, vrows, zeroed = (
            k.sem(x) for x in ("q_prod", "q_int", "q_done", "diag_ok", "row_ps", "v_prod", "v_scaled", "v_int", "v_done", "vrows", "v_zeroed"))
        with nc.Block() as block:
            @block.tensor
            def _(pe):
                pe.wait_ge(diag_ok, 1)
                for j in range(2):
                    for t in range(3):
                        mm = pe.matmul(pv[:, j, t * P:(t + 1) * P], ones[:, :], diag[:, j, t, :], start=True, stop=True)
                mm.then_inc(row_ps, 1)
                with pe.Fori(0, NCH) as i:
                    for u in range(2):
                        pe.wait_ge(q_int, i * 6 + 3 * u + 3)
                        for t in range(3):
                            for kt in range(2):
                                mm = pe.matmul(pq[:, u, t, 0:W], wqT[:, kt, (3 * u + t) * P:(3 * u + t + 1) * P],
                                               xqT[:, kt, ds(i * W, W)], start=(kt == 0), stop=(kt == 1))
                        mm.then_inc(q_prod, 1)
                pe.wait_ge(vrows, 1)

                def v_product(buf, w, lhs):
                    for kt in range(2):
                        mm = pe.matmul(pv[:, buf, w * C:(w + 1) * C], lhs(kt), heads16(wqT, kt, 24, H), start=(kt == 0), stop=(kt == 1))
                    return mm

                with pe.Fori(0, B // 4) as i:
                    for u in range(2):
                        pe.wait_ge(v_scaled, i * 2 + u + 1)
                        for w in range(2):
                            mm = v_product(u, w, lambda kt: xqT[:, kt, ds(i * 4 * N + (2 * u + w) * N, NT)])
                        mm.then_inc(v_prod, 1)
                for u in range(G // 2):
                    pe.wait_ge(v_scaled, B // 2 + u + 1)
                    for w in range(2):
                        mm = v_product(u % 2, w, lambda kt: xqI[:, kt, (2 * u + w) * P:(2 * u + w + 1) * P])
                    mm.then_inc(v_prod, 1)

            @block.scalar
            def _(act):
                with act.Fori(0, NCH) as i:
                    for u in range(2):
                        act.wait_ge(q_prod, i * 2 + u + 1)
                        act.wait_ge(q_done, i * 6 + 3 * u + 3)
                        for t in range(3):
                            j = 3 * u + t
                            act.activation(qi[:, u, t, :], pq[:, u, t, 0:W], ACT.Identity, scale=m["ap"][:, j:j + 1],
                                           bias=m["biasp"][:, j:j + 1]).then_inc(q_int, 1)

            @block.gpsimd
            def _(pool):
                pool.memset(vt[:, :, :], 0.0).then_inc(zeroed, 1)
                pool.memset(vi[:, :, :], 0.0).then_inc(zeroed, 1)
                pool.sem_inc(q_done, 6)

            @block.vector
            def _(v):
                link = chained(v, k.sem("v_chain"))
                v.sem_inc(q_int, 6)
                v.sem_inc(v_scaled, 2)
                cap = m["qh"][:, 3:4]
                link(v.memset(ones[:, :], 1.0))
                for j, col in enumerate((m["ap"], m["biasp"])):
                    for t in range(3):
                        link(v.tensor_scalar(diag[:, j, t, :], ident[:, :], col[:, 6 + t:7 + t], None, ALU.mult))
                v.sem_inc(diag_ok, 1)
                v.wait_ge(row_ps, 1)
                for j in range(2):
                    v.tensor_copy(rows[:, j, :].rearrange("p (h f) -> p h f", f=HD),
                                  pv[:, j, 0:3 * P].rearrange("p (h f) -> p h f", f=32)[:, :, 0:HD]).then_inc(vrows, 1)
                with v.Fori(0, NCH) as i:
                    for u in range(2):
                        for t in range(3):
                            v.wait_ge(q_int, i * 6 + 3 * u + t + 7)
                            v.tensor_scalar(qk[:, ds(i * 2, 2), 3 * u + t, :], qi[:, u, t, :].rearrange("p (b n) -> p b n", n=N), cap, None, ALU.min).then_inc(q_done, 1)
                v.wait_ge(zeroed, 2)
                v.wait_ge(vrows, 2)
                both = lambda j: rows[:, j, :].unsqueeze(1).to_broadcast([P, 2, C])

                def v_quant(u, n, out):
                    v.wait_ge(v_prod, n + 1)
                    v.tensor_tensor(vf[:, u, :, :], pv[:, u, 0:2 * C].rearrange("p (w c) -> p w c", c=C), both(0), ALU.mult).then_inc(v_scaled, 1)
                    v.wait_ge(v_scaled, n + 3)
                    v.tensor_tensor(v16[:, u, :, :], vf[:, u, :, :], both(1), ALU.add).then_inc(v_int, 1)
                    v.wait_ge(v_int, n + 1)
                    v.tensor_scalar(out.rearrange("p w (h f) -> p (w h) f", f=32)[:, :, 0:HD],
                                    v16[:, u, :, :].rearrange("p w (h f) -> p (w h) f", f=HD), cap, None, ALU.min).then_inc(v_done, 1)

                with v.Fori(0, B // 4) as i:
                    for u in range(2):
                        v_quant(u, i * 2 + u, vt[:, ds(i * 4 + 2 * u, 2), :])
                for u in range(G // 2):
                    v_quant(u % 2, B // 2 + u, vi[:, 2 * u:2 * u + 2, :])
                v.wait_ge(v_done, (B + G) // 2)
                for j in range(4):
                    v.memset(vi[32 * j:32 * j + ID, :, :], 0.0)


class Stage:

    def __init__(self, k, sb, m, name, placing):
        self.m, self.placing = m, placing
        self.kb, self.qb = sb(name + "_kb", [P, 2, HT, 4, N], BF16), sb(name + "_qb", [P, 2, HT, 4, 32], BF16)
        self.loaded = [k.sem(f"{name}_loaded{i}") for i in range(2)]
        self.placed, self.zeroed, self.scored = k.sem(name + "_placed"), k.sem(name + "_zeroed"), k.sem(name + "_scored")

    def clear(self, pool):
        pool.memset(self.kb[:, :, :, :, :], 0.0).then_inc(self.zeroed, 1)
        pool.memset(self.qb[:, :, :, :, :], 0.0).then_inc(self.zeroed, 1)
        pool.wait_ge(self.zeroed, 2)

    def free(self, eng, n, u):
        if not (isinstance(n, int) and n < 2):
            eng.wait_ge(self.scored, (n - 1) * (RT // 3))

    def load(self, sp, n, u):
        self.free(sp, n, u)
        for j in range(4):
            r = slice(32 * j, 32 * j + 32)
            sp.dma_start(self.kb[r, u, :, j, :], self.m["qk"][r, n, HT:2 * HT, :]).then_inc(self.loaded[u], 16)
            if not self.placing:
                sp.dma_start(self.qb[r, u, :, j, :], self.m["qk"][r, n, 0:HT, IW:N]).then_inc(self.loaded[u], 16)

    def place(self, pool, n, u):
        self.free(pool, n, u)
        for j in range(4):
            r = slice(32 * j, 32 * j + 32)
            ins = pool.tensor_copy(self.qb[r, u, :, j, :], self.m["qk"][r, n, 0:HT, IW:N])
        ins.then_inc(self.placed, 1)

    def ready(self, pe, n, half, u):
        pe.wait_ge(self.loaded[u], (half + 1) * (64 if self.placing else 128))
        if self.placing:
            pe.wait_ge(self.placed, n + 1)

    def scores(self, pe, n, u, i, banks):
        qk = self.m["qk"]
        for w in range(3):
            t, j = divmod(3 * i + w, 4)
            lhs, rhs = (qk[:, n, t, 0:NT], self.kb[:, u, t, j, :]) if t < HT else \
                (self.qb[:, u, w, :, :].rearrange("p j n -> p (j n)"), qk[:, n, HT + w, :])
            mm = pe.matmul(banks[:, i, w * N:(w + 1) * N], lhs, rhs, start=True, stop=True)
        mm.then_inc(self.scored, 1)


def range_scores(k, m):
    NB = RT // 3
    with ExitStack() as st:
        sb = lambda n, s, t=F32: k.sb(n, s, t, st)
        s = Stage(k, sb, m, "rs", True)
        low = sb("score_low", [P, B, RT])
        rmax, con = m["rmax"], m["con"]
        mm1, mm2 = sb("sm1", [P, 2]), sb("sm2", [P, 2])
        banks = k.ps("rs_banks", [P, NB, 512], F32, st)
        reduced, bank_used, sr, sred, vbd_zero = (k.sem(x) for x in ("rs_reduced", "rs_bank_used", "rs_r", "rs_red", "vbd_zero"))
        vbd = m["vbd"]
        with k.nc.Block() as block:
            @block.gpsimd
            def _(pool):
                s.clear(pool)
                s.place(pool, 0, 0)
                s.place(pool, 1, 1)
                with pool.Fori(1, B // 2) as i:
                    for u in range(2):
                        s.place(pool, i * 2 + u, u)
                pool.wait_ge(sr, 1)
                pool.partition_all_reduce(mm2[:, :], mm1[:, :], P, RMAX).then_inc(sred, 1)

            @block.sync
            def _(sp):
                sp.wait_ge(s.zeroed, 2)
                s.load(sp, 0, 0)
                s.load(sp, 1, 1)
                with sp.Fori(1, B // 2) as i:
                    for u in range(2):
                        s.load(sp, i * 2 + u, u)

            @block.scalar
            def _(act):
                act.wait_ge(vbd_zero, 1)
                for c in range(4):
                    for j in range(4):
                        dst = vbd.rearrange("p (g c) t j f -> p g c t j f", c=4)[32 * j:32 * j + 32, :, c, :, j, :]
                        src = m["vi"].rearrange("p g (t j f) -> p g t j f", j=4, f=32)[32 * c:32 * c + 32, :, :, j, :]
                        act.activation(dst, src, ACT.Copy)

            @block.tensor
            def _(pe):
                with pe.Fori(0, B // 2) as i:
                    for u in range(2):
                        n = i * 2 + u
                        s.ready(pe, n, i, u)
                        for b in range(NB):
                            pe.wait_ge(bank_used, n * NB + b + 1)
                            s.scores(pe, n, u, b, banks)

            @block.vector
            def _(v):
                link = chained(v, k.sem("rs_chain"))
                v.sem_inc(bank_used, NB)
                v.memset(vbd[:, :, :, :, :], 0.0).then_inc(vbd_zero, 1)
                with v.Fori(0, B // 2) as i:
                    for u in range(2):
                        n = i * 2 + u
                        for b in range(NB):
                            tiles = banks[:, b, 0:3 * N].rearrange("p (w n) -> p w n", n=N)
                            v.wait_ge(s.scored, n * NB + b + 1)
                            v.tensor_reduce(rmax[:, n, 3 * b:3 * b + 3], tiles, AX, ALU.max).then_inc(reduced, 1)
                            v.tensor_reduce(low[:, n, 3 * b:3 * b + 3], tiles, AX, ALU.min).then_inc(bank_used, 1)
                v.wait_ge(reduced, B * NB)
                v.wait_ge(bank_used, (B + 1) * NB)
                flat = lambda x: x[:, :, :].rearrange("p b t -> p (b t)")
                link(v.tensor_reduce(mm1[:, 0:1], flat(rmax), AX, ALU.max))
                link(v.tensor_reduce(mm1[:, 1:2], flat(low), AX, ALU.min, negate=True))
                qh, qa = m["qh"], m["qa"]
                link(v.tensor_tensor(con[:, 0:1], qh[:, 0:1], qh[:, 0:1], ALU.mult))
                link(v.tensor_scalar(con[:, 0:1], con[:, 0:1], HD ** -0.5, None, ALU.mult))
                v.tensor_scalar(mm1[:, :], mm1[:, :], con[:, 0:1], None, ALU.mult).then_inc(sr, 1)
                v.wait_ge(sred, 1)
                quant_params(v, link, mm2, qa)
                inv = qa[:, 1:2]
                c = lambda i: con[:, i:i + 1]
                link(v.tensor_scalar(c(0), c(0), inv, None, ALU.mult))
                link(v.tensor_scalar(c(1), inv, 0.6931, 0.5, ALU.mult, ALU.add))
                link(v.tensor_scalar(c(1), c(1), ROUND, ROUND, ALU.add, ALU.subtract))
                link(v.tensor_scalar(c(2), c(1), -30.0, None, ALU.mult))
                link(v.reciprocal(c(4), c(1)))
                link(v.tensor_scalar(c(3), c(4), -1.0, None, ALU.mult))
                link(v.tensor_scalar(c(4), c(4), 0.5, 0.5, ALU.mult, ALU.subtract))
                link(v.tensor_scalar(c(5), inv, 0.96963238 / 0.35815147, 0.5, ALU.mult, ALU.subtract))
                link(v.tensor_scalar(c(5), c(5), ROUND, ROUND, ALU.add, ALU.subtract))
                link(v.tensor_scalar(c(5), c(5), 0.5, None, ALU.mult))
                link(v.tensor_tensor(c(6), inv, inv, ALU.mult))
                link(v.tensor_scalar(c(6), c(6), 1.0 / 0.35815147, 0.5, ALU.mult, ALU.subtract))
                link(v.tensor_scalar(c(6), c(6), ROUND, ROUND, ALU.add, ALU.subtract))
                link(v.tensor_tensor(c(7), c(5), c(5), ALU.mult))
                link(v.tensor_tensor(c(7), c(6), c(7), ALU.subtract))
                link(v.tensor_scalar(flat(rmax), flat(rmax), c(0), None, ALU.mult))
                link(v.tensor_scalar(flat(rmax), flat(rmax), ROUND, ROUND, ALU.add, ALU.subtract))
                link(v.tensor_scalar(flat(rmax), flat(rmax), qa[:, 3:4], None, ALU.min))


def attention(k, m):
    NB = RT // 3
    LAG_E, LAG_P, LAG_T, LAG_V = 2, 3, 5, 6
    with ExitStack() as st:
        sb = lambda n, s, t=F32: k.sb(n, s, t, st)
        s = Stage(k, sb, m, "at", False)
        qk, vt, vbd, con, rmax, identb = (m[x] for x in ("qk", "vt", "vbd", "con", "rmax", "identb"))
        x, qf = (sb(y, [P, NB, 3, N], I16) for y in ("logit", "octave"))
        xb = lambda b: x[:, b].bitcast(BF16)
        tr = sb("rest", [P, NB, 3, N], BF16)
        pw = sb("pow2", [P, NB, 3, N], I16)
        ex, w = sb("expo", [P, NB, 3, N]), sb("weight", [P, NB, 3, N])
        tot, inv, cap = sb("total", [P, NB, 3]), sb("inv_total", [P, NB, 3]), sb("top_weight", [P, NB, 3])
        pt, pi = sb("p_text", [P, RT, P], BF16), sb("p_image", [P, RT, 32], BF16)
        ptT, piT, pjT = sb("pT_text", [P, H, N], BF16), sb("pT_image", [P, HT, P], BF16), sb("pT_both", [P, HT, 32], BF16)
        vs = sb("v_stage", [P, 3 * P], BF16)
        ph = sb("p_bits", [P, NB, 3, N], I16)
        v_start, pf_done, passed = k.sem("at_start"), k.sem("at_pf_done"), k.sem("at_passed")
        banks, pT, po = k.ps("at_banks", [P, NB, 512], F32, st), k.ps("at_pT", [P, 2, 1024], BF16, st), k.ps("at_out", [P, 512], F32, st)
        sem = lambda *names: (k.sem("at_" + y) for y in names)
        x_raw, x_done, q_done, t_done, pw_done, r_done, sq_done, e_done = sem("x_raw", "x_done", "q_done", "t_done", "pw_done", "r_done", "sq_done", "e_done")
        s1, s2, s3, s4, w_done, ph_done, y_done, p_done, c_done = sem("s1", "s2", "s3", "s4", "w_done", "ph_done", "y_done", "p_done", "c_done")
        tr_done, ev_done, pj_done, pv_done, out_done, vs_done = sem("tr_done", "ev_done", "pj_done", "pv_done", "out_done", "vs_done")

        def steps(eng, body):
            for kk in range(2 * NB):
                body(0, kk)
            with eng.Fori(1, B // 2) as i:
                for kk in range(2 * NB):
                    body(i, kk)
            for kk in range(2 * NB, 2 * NB + LAG_V + 1):
                body(B // 2 - 1, kk)

        def bank(c, kk, lag):
            kk -= lag
            if isinstance(c, int) and (c * 2 * NB + kk < 0 or c * 2 * NB + kk >= B * NB):
                return None
            return c * 2 + kk // NB, kk % NB, c * (2 * NB) + kk, (kk // NB) % 2, c + kk // (2 * NB)

        with k.nc.Block() as block:
            @block.sync
            def _(sp):
                sp.wait_ge(s.zeroed, 2)
                s.load(sp, 0, 0)
                s.load(sp, 1, 1)
                with sp.Fori(1, B // 2) as i:
                    for u in range(2):
                        s.load(sp, i * 2 + u, u)

            @block.tensor
            def _(pe):
                pe.wait_ge(v_start, 1)

                def body(c, kk):
                    if (y := bank(c, kk, 0)) is not None:
                        n, b, num, u, half = y
                        if b == 0:
                            s.ready(pe, n, half, u)
                        pe.wait_ge(x_raw, num + 1)
                        s.scores(pe, n, u, b, banks)
                    if (y := bank(c, kk, LAG_T)) is not None:
                        n, b, num, u, half = y
                        pe.wait_ge(c_done, num + 1)
                        pe.wait_ge(ev_done, num + 1)
                        for j in range(3):
                            mm = pe.transpose(pT[:, (kk - LAG_T) % 2, j * P:(j + 1) * P], pt[:, 3 * b + j, :], identb[:, :])
                        if b == NB - 1:
                            for t in range(HT):
                                mm = pe.transpose(pT[:, (kk - LAG_T) % 2, (3 + t) * P:(4 + t) * P], pi[:, 4 * t:4 * t + 4, :].rearrange("p j n -> p (j n)"), identb[:, :])
                        mm.then_inc(tr_done, 1)
                    y = bank(c, kk, LAG_V)
                    if y is not None and y[1] == NB - 1:
                        n = y[0]
                        pe.wait_ge(ev_done, n * NB + NB + 2)
                        pe.wait_ge(pj_done, n + 1)
                        pe.wait_ge(vs_done, n + 1)
                        pe.wait_ge(out_done, n + 1)
                        for t in range(HT):
                            lhs = vbd[:, n, t, :, :].rearrange("p j f -> p (j f)")
                            pe.matmul(po[:, t * N:t * N + NT], lhs, piT[:, t, :], start=(t == 0), stop=False, skip_group_check=True)
                            pe.matmul(po[:, t * N + NT:(t + 1) * N], lhs, pjT[:, t, ID:32], start=False, stop=False, skip_group_check=True)
                            for j in range(4):
                                h = 4 * t + j
                                mm = pe.matmul(po[32 * j:32 * j + 32, t * N:(t + 1) * N], vs[:, h * 32:h * 32 + 32], ptT[:, h, :],
                                               start=False, stop=(h == H - 1), skip_group_check=True)
                        mm.then_inc(pv_done, 1)
                steps(pe, body)

            @block.gpsimd
            def _(pool):
                s.clear(pool)

                def body(c, kk):
                    if (y := bank(c, kk, 0)) is not None:
                        n, b, num, u, half = y
                        sl = (slice(None), b)
                        wait_apart(pool, q_done, num + 1, passed)
                        pool.tensor_scalar(tr[sl], qf[sl], con[:, 1:2], 0.0, ALU.mult, ALU.add).then_inc(t_done, 1)
                        pool.tensor_scalar(pw[sl], qf[sl], -128.0, 127.0 * 128.0, ALU.mult, ALU.add).then_inc(pw_done, 1)
                        pool.wait_ge(t_done, num + 1)
                        pool.tensor_tensor(tr[sl], tr[sl], xb(b), ALU.add).then_inc(r_done, 1)
                    y = bank(c, kk, LAG_V - 1)
                    if y is not None and y[1] == 2:
                        n = y[0]
                        pool.wait_ge(pv_done, n + 1)
                        pool.tensor_copy(vs[:, :], vt[:, n, :]).then_inc(vs_done, 1)
                steps(pool, body)

            @block.scalar
            def _(act):
                act.sem_inc(ev_done, 2)
                act.sem_inc(out_done, 1)

                def body(c, kk):
                    if (y := bank(c, kk, 1)) is not None:
                        n, b, num, u, half = y
                        act.wait_ge(r_done, num + 1)
                        act.activation(ex[:, b], tr[:, b], ACT.Square, bias=con[:, 5:6]).then_inc(sq_done, 1)
                    y = bank(c, kk, LAG_V)
                    if y is not None and y[1] == NB - 1:
                        n = y[0]
                        act.wait_ge(pv_done, n + 2)
                        act.activation(out_f32(m)[:, n, :], po[:, 0:HT * N], ACT.Copy).then_inc(out_done, 1)
                    if (y := bank(c, kk, LAG_T)) is not None:
                        n, b, num, u, half = y
                        act.wait_ge(tr_done, num + 1)
                        act.wait_ge(pv_done, n + 1)
                        tiles = pT[:, (kk - LAG_T) % 2, 0:6 * P].rearrange("p (j n) -> p j n", n=P)
                        if b < NB - 1:
                            act.activation(ptT[:, 3 * b:3 * b + 3, 0:NT], tiles[:, 0:3, :], ACT.Copy).then_inc(ev_done, 1)
                        else:
                            act.activation(ptT[:, :, NT:N], pT[:, (kk - LAG_T) % 2, 0:3 * P].rearrange("p (h n) -> p h n", n=32)[:, :, ID:32], ACT.Copy)
                            act.activation(piT[:, :, :], tiles[:, 3:6, :], ACT.Copy).then_inc(ev_done, 1)
                steps(act, body)

            @block.vector
            def _(v):
                v.sem_inc(x_raw, NB)
                v.sem_inc(pv_done, 1)
                v.sem_inc(v_start, 1)

                def body(c, kk):
                    ya, ye, yp = bank(c, kk, 0), bank(c, kk, LAG_E), bank(c, kk, LAG_P)
                    if ya is not None:
                        n, b, num, u, half = ya
                        v.wait_ge(s.scored, num + 1)
                        v.scalar_tensor_tensor(x[:, b], banks[:, b, 0:3 * N].rearrange("p (w n) -> p w n", n=N), con[:, 0:1],
                                               rmax[:, n, 3 * b:3 * b + 3].unsqueeze(2).to_broadcast([P, 3, N]), ALU.mult, ALU.subtract).then_inc(x_raw, 1)
                    if ye is not None:
                        _, be, numE, _, _ = ye
                        v.wait_ge(sq_done, numE + 1)
                        v.wait_ge(pw_done, numE + 1)
                        for j in range(3):
                            ins = v.scalar_tensor_tensor(ex[:, be, j], ex[:, be, j], con[:, 7:8], pw[:, be, j].bitcast(BF16),
                                                         ALU.add, ALU.mult, accum_out=tot[:, be, j:j + 1])
                        ins.then_inc(e_done, 1)
                    if ya is not None:
                        v.wait_ge(x_raw, num + 1 + NB)
                        v.tensor_scalar(xb(b), x[:, b], con[:, 2:3], 0.0, ALU.max, ALU.min).then_inc(x_done, 1)
                    if yp is not None:
                        _, bp, numP, _, _ = yp
                        high = w[:, bp].rearrange("p w n -> p (w n)").bitcast(I16).rearrange("p (n two) -> p n two", two=2)[:, :, 1]
                        flat = lambda a: a[:, bp].rearrange("p w n -> p (w n)")
                        v.wait_ge(w_done, numP + 1)
                        v.tensor_scalar(flat(ph), high, -128, None, ALU.bitwise_and).then_inc(ph_done, 1)
                    if ye is not None:
                        v.wait_ge(e_done, numE + 1)
                        v.tensor_scalar(tot[:, be], tot[:, be], 1.0, None, ALU.max).then_inc(s1, 1)
                    if ya is not None:
                        v.wait_ge(x_done, num + 1)
                        v.tensor_scalar(qf[:, b], xb(b), con[:, 3:4], con[:, 4:5], ALU.mult, ALU.add).then_inc(q_done, 1)
                    if ye is not None:
                        v.wait_ge(s1, numE + 1)
                        v.reciprocal(inv[:, be], tot[:, be]).then_inc(s2, 1)
                    if yp is not None:
                        v.wait_ge(ph_done, numP + 1)
                        v.scalar_tensor_tensor(flat(w), flat(ph).bitcast(BF16), 1.5, flat(w), ALU.add, ALU.mult).then_inc(y_done, 1)
                    if ye is not None:
                        v.wait_ge(s2, numE + 1)
                        v.tensor_scalar(cap[:, be], inv[:, be], con[:, 6:7], 2.0 / 3.0, ALU.mult, ALU.is_gt).then_inc(s3, 1)
                        v.wait_ge(s3, numE + 1)
                        v.tensor_scalar(cap[:, be], cap[:, be], 0.5, 0.5 - 2.0 ** -24, ALU.mult, ALU.add).then_inc(s4, 1)
                    if yp is not None:
                        v.wait_ge(y_done, numP + 1)
                        v.tensor_scalar(flat(ph), high, -128, None, ALU.bitwise_and).then_inc(p_done, 1)
                    if ye is not None:
                        v.wait_ge(s4, numE + 1)
                        for j in range(3):
                            ins = v.tensor_scalar(w[:, be, j], ex[:, be, j], inv[:, be, j:j + 1], cap[:, be, j:j + 1], ALU.mult, ALU.min)
                        ins.then_inc(w_done, 1)
                    if yp is not None:
                        v.wait_ge(p_done, numP + 1)
                        if not (isinstance(c, int) and c * 2 * NB + kk - LAG_P < NB):
                            v.wait_ge(tr_done, numP - bp)
                        pb = ph[:, bp].bitcast(BF16)
                        v.tensor_scalar(pi[:, 3 * bp:3 * bp + 3, :], pb[:, :, IW:N], 384.0, 384.0, ALU.add, ALU.subtract).then_inc(pf_done, 1)
                        v.tensor_scalar(pt[:, 3 * bp:3 * bp + 3, :], pb[:, :, 0:NT], 384.0, 384.0, ALU.add, ALU.subtract).then_inc(c_done, 1)
                        if bp == NB - 1:
                            v.wait_ge(pf_done, numP + 1)
                            v.wait_ge(pv_done, yp[0] + 1)
                            v.transpose(pjT[:, :, :].rearrange("p t n -> p (t n)"), pi[:, H:RT, :].rearrange("p t n -> p (t n)")).then_inc(pj_done, 1)
                steps(v, body)


def out_f32(m):
    return m["qkflat"].bitcast(F32).rearrange("p (b n) -> p b n", b=B)


def project(k, m):
    Hres, ident, identb, qh, qo, qp = (m[x] for x in ("H", "ident", "identb", "qh", "qo", "qp"))
    CH = B // 2
    with ExitStack() as st:
        sb = lambda n, s, t=F32: k.sb(n, s, t, st)
        wraw, w16, wb = sb("pj_w", [P, 2, HT * P]), sb("pj_w16", [P, 2, HT * P], I16), sb("pj_wb", [P, 2, HT * P], BF16)
        wT = sb("pj_wT", [P, HT, 2 * P], BF16)
        ws, wi, ones, diag = sb("pj_ws", [P, 2]), sb("pj_wi", [P, 2]), sb("pj_ones", [P, P]), sb("pj_diag", [P, 2, P])
        row, brow, pad = sb("pj_row", [P, C]), sb("pj_brow", [P, C]), sb("pj_pad", [P, 2])
        mm = [sb(f"pj_mm{i}", [P, 2]) for i in range(4)]
        inv = sb("pj_inv", [P, 1])
        o16, oT, oI = sb("pj_o16", [P, 2, 2, HT * N], I16), sb("pj_oT", [P, HT, B, N], BF16), sb("pj_oI", [P, HT, G * P], BF16)
        Y = sb("pj_Y", [P, NTILE, C])
        pw, pr, py = k.ps("pj_pw", [P, 1024], BF16, st), k.ps("pj_pr", [P, 512], F32, st), k.ps("pj_py", [P, 4, 512], F32, st)
        loaded, wready, wps, wdone, rps, red, redd, oq, y_acc, y_mul, y_out = (
            k.sem("pj_" + x) for x in ("loaded", "wready", "wps", "wdone", "rps", "red", "redd", "oq", "y_acc", "y_mul", "y_out"))
        real = out_f32(m)
        with k.nc.Block() as block:
            @block.sync
            def _(sp):
                sp.dma_start(wraw[:, :, :], k.d["wproj"]).then_inc(loaded, 16)
                sp.dma_start(brow[:, :], k.d["projb"]).then_inc(loaded, 16)
                sp.dma_start(pad[:, :], k.d["pad"]).then_inc(loaded, 16)

            @block.gpsimd
            def _(pool):
                for i in range(2):
                    pool.wait_ge(red, i + 1)
                    pool.partition_all_reduce(mm[2 * i + 1][:, :], mm[2 * i][:, :], P, RMAX).then_inc(redd, 1)

            @block.tensor
            def _(pe):
                pe.wait_ge(wready, 1)
                for t in range(HT):
                    for q in range(2):
                        x = pe.transpose(pw[:, (t * 2 + q) * P:(t * 2 + q + 1) * P], wb[:, q, t * P:(t + 1) * P], identb[:, :])
                x.then_inc(wps, 1)
                for q in range(2):
                    x = pe.matmul(pr[:, q * P:q * P + CK[q]], ones[:, :], diag[:, q, 0:CK[q]], start=True, stop=True)
                x.then_inc(rps, 1)
                pe.wait_ge(wdone, 1)

                def product(slot, w, lhs):
                    for t in range(HT):
                        x = pe.matmul(py[:, slot, w * C:(w + 1) * C], lhs(t), wT[:, t, 0:C], start=(t == 0), stop=(t == HT - 1))
                    return x

                pe.wait_ge(oq, CH + 1)
                with pe.Fori(0, B // 4) as i:
                    for u in range(2):
                        pe.wait_ge(y_mul, i * 2 + u + 1)
                        for w in range(2):
                            x = product(u, w, lambda t: oT[:, t, i * 4 + 2 * u + w, 0:NT])
                        x.then_inc(y_acc, 1)
                pe.wait_ge(oq, CH + 2)
                for g in range(G // 2):
                    pe.wait_ge(y_mul, B // 2 + g + 1)
                    for w in range(2):
                        x = product(g % 2, w, lambda t: oI[:, t, (2 * g + w) * P:(2 * g + w + 1) * P])
                    x.then_inc(y_acc, 1)

            @block.vector
            def _(v):
                link = chained(v, k.sem("pj_chain"))
                link(v.memset(ones[:, :], 1.0))
                v.wait_ge(loaded, 48)
                link(v.tensor_reduce(ws[:, :], wraw[:, :, :], AX, ALU.max, apply_absolute_value=True))
                link(v.tensor_scalar(ws[:, :], ws[:, :], 1e-8, 1.0 / 127.0, ALU.max, ALU.mult))
                link(v.reciprocal(wi[:, :], ws[:, :]))
                for q in range(2):
                    link(v.tensor_scalar(diag[:, q, :], ident[:, :], ws[:, q:q + 1], None, ALU.mult))
                    link(v.tensor_scalar(w16[:, q, :], wraw[:, q, :], wi[:, q:q + 1], None, ALU.mult))
                v.tensor_scalar(wb[:, :, :], w16[:, :, :], -128.0, 127.0, ALU.max, ALU.min).then_inc(wready, 1)
                flat = m["qkflat"].bitcast(F32)
                link(v.tensor_reduce(mm[0][:, 0:1], flat, AX, ALU.max))
                link(v.tensor_reduce(mm[0][:, 1:2], flat, AX, ALU.min, negate=True))
                link(v.tensor_scalar(mm[0][:, :], mm[0][:, :], qh[:, 0:1], None, ALU.mult))
                v.tensor_tensor(mm[0][:, :], mm[0][:, :], pad[:, :], ALU.min).then_inc(red, 1)
                v.wait_ge(wps, 1)
                v.tensor_copy(wT[:, :, :].rearrange("p t n -> p (t n)"), pw[:, 0:HT * 2 * P]).then_inc(wdone, 1)
                v.wait_ge(redd, 1)
                quant_params(v, link, mm[1], qo)
                link(v.tensor_tensor(inv[:, :], qo[:, 1:2], qh[:, 0:1], ALU.mult))
                v.wait_ge(rps, 1)
                link(v.tensor_scalar(row[:, :], pr[:, 0:C], qo[:, 0:1], None, ALU.mult))
                o_int = k.sem("pj_o_int")
                v.sem_inc(oq, 1)
                with v.Fori(0, CH // 2) as i:
                    for u in range(2):
                        b2 = i * 4 + 2 * u
                        n = i * 2 + u
                        v.wait_ge(oq, n + 1)
                        v.tensor_scalar(o16[:, u, :, :], real[:, ds(b2, 2), :], inv[:, 0:1], qo[:, 3:4], ALU.mult, ALU.min).then_inc(o_int, 1)
                        v.wait_ge(o_int, n + 1)
                        v.tensor_copy(oT[:, :, ds(b2, 2), :].rearrange("p t b n -> p b t n"), o16[:, u, :, :].rearrange("p b (t n) -> p b t n", t=HT)).then_inc(oq, 1)
                v.wait_ge(oq, CH + 1)
                for t in range(HT):
                    ins = v.tensor_copy(oI[:, t, :].rearrange("p (b n) -> p b n", n=32), oT[:, t, :, IW:N])
                ins.then_inc(oq, 1)
                v.sem_inc(y_mul, 2)
                both = lambda r: r[:, :].unsqueeze(1).to_broadcast([P, 2, C])

                def collect(slot, n, out):
                    v.wait_ge(y_acc, n + 1)
                    v.tensor_tensor(out, py[:, slot, 0:2 * C].rearrange("p (w c) -> p w c", c=C), both(row), ALU.mult).then_inc(y_mul, 1)
                    v.wait_ge(y_mul, n + 3)
                    v.tensor_tensor(out, out, both(brow), ALU.add).then_inc(y_out, 1)

                with v.Fori(0, B // 4) as i:
                    for u in range(2):
                        collect(u, i * 2 + u, Y[:, ds(i * 4 + 2 * u, 2), :])
                for g in range(G // 2):
                    collect(g % 2, B // 2 + g, Y[:, B + 2 * g:B + 2 * g + 2, :])
                v.wait_ge(y_out, (B + G) // 2)
                flat = lambda a: a[:, :, :].rearrange("p t c -> p (t c)")
                link(v.tensor_reduce(mm[2][:, 0:1], flat(Y), AX, ALU.max))
                link(v.tensor_reduce(mm[2][:, 1:2], flat(Y), AX, ALU.min, negate=True))
                v.sem_inc(red, 1)
                v.wait_ge(redd, 2)
                quant_params(v, link, mm[3], qp)
                y16 = oT[:, :, :, :].rearrange("p t b n -> p (t b n)")[:, 0:NTILE * C].bitcast(I16)
                link(v.tensor_scalar(y16, flat(Y), qp[:, 1:2], qp[:, 3:4], ALU.mult, ALU.min))
                link(v.scalar_tensor_tensor(flat(Hres), y16, qp[:, 0:1], flat(Hres), ALU.mult, ALU.add))


def norm_stats(v, rows, stat, mv4, mv, groups, sem):
    stats, aggr, kept, passed = sem
    v.sem_inc(kept, 1)
    with v.Fori(0, groups) as g:
        wait_apart(v, kept, g + 1, passed)
        for w in range(4):
            v.bn_stats(stat[:, w, :], rows[:, g * 4 + w, :]).then_inc(stats, 1)
        for w in range(4):
            wait_apart(v, stats, g * 4 + w + 1, passed)
            v.bn_aggr(mv4[:, w, :], stat[:, w, :]).then_inc(aggr, 1)
        v.wait_ge(aggr, g * 4 + 4)
        v.tensor_copy(mv[:, ds(g * 4, 4), :], mv4[:, :, :]).then_inc(kept, 1)
    v.wait_ge(kept, groups + 1)


def ffn_inputs(k, m):
    d, Hres, ident = k.d, m["H"], m["ident"]
    xh, xl, w1h, w1l, w2h, w2l, sel, gw, gwi = (m[x] for x in ("xh", "xl", "w1h", "w1l", "w2h", "w2l", "sel", "gw", "gwi"))
    with ExitStack() as st:
        sb = lambda n, s, t=F32: k.sb(n, s, t, st)
        w1, w2, wg = sb("f_w1", [P, 2, E, FF]), sb("f_w2", [P, E, FT, C]), sb("f_wg", [P, 2, E])
        stat, mv4, mv = sb("f_stat", [P, 4, 6]), sb("f_mv4", [P, 4, 2]), sb("f_mv", [P, NTILE, 2])
        rstd, root, newt = sb("f_rstd", [P, NTILE]), sb("f_root", [P, NTILE]), sb("f_newt", [P, NTILE])
        xn = sb("f_xn", [P, 2, 4, C])
        sums, sumx, gp, ones = sb("f_sums", [P, 2, 2, B]), sb("f_sum", [P, 2, B]), sb("f_gp", [P, 2, E, B]), sb("f_ones", [P, P])
        lg, mx, tot, hit, one = sb("f_lg", [P, E, B]), sb("f_mx", [P, B]), sb("f_tot", [P, B]), sb("f_hit", [P, 2, B]), sb("f_one", [P, B])
        ptx, pim, pg = k.ps("f_ptx", [P, 2, 512], F32, st), k.ps("f_pim", [P, 2, 512], F32, st), k.ps("f_pg", [P, 512], F32, st)
        loaded, var, rooted, xn_done, xt_ps, xt_hi, xt_out, zeroed, gready, gps, eready, edone = (
            k.sem("f_" + x) for x in ("loaded", "var", "rooted", "xn_done", "xt_ps", "xt_hi", "xt_out", "zeroed", "gready", "gps", "eready", "edone"))
        w_hi, st_sems = k.sem("f_w_hi"), [k.sem("f_st" + x) for x in ("stats", "aggr", "kept", "passed")]
        text = lambda a, kt, g: a[0:CK[kt], kt, ds(g * (4 * N), 4 * N)].rearrange("p (v n) -> p v n", n=N)[:, :, 0:NT]
        image = lambda a, kt, g: a[0:CK[kt], kt, ds(g * (4 * N), 4 * N)].rearrange("p (v n) -> p v n", n=N)[:, :, NT:N]
        ptext = lambda kt: ptx[0:CK[kt], kt, :].rearrange("p (v n) -> p v n", n=P)
        pimage = lambda kt: pim[0:CK[kt], kt, 0:P].rearrange("p (v n) -> p v n", n=32)[:, :, ID:32]
        halves = ((text, ptext), (image, pimage))
        with k.nc.Block() as block:
            @block.sync
            def _(sp):
                sp.dma_start(w1[:, :, :, :], d["w1"]).then_inc(loaded, 16)
                sp.dma_start(w2[:, :, :, :], d["w2"]).then_inc(loaded, 16)
                sp.dma_start(wg[:, :, :], d["wg"]).then_inc(loaded, 16)
                sp.dma_start(m["b2"][:, :, :], d["b2"]).then_inc(loaded, 16)
                sp.dma_start(m["b2c"][:, :, :], d["b2c"]).then_inc(loaded, 16)

            @block.gpsimd
            def _(pool):
                pool.memset(xh[64:P, 1, :], 0.0).then_inc(zeroed, 1)
                pool.memset(xl[64:P, 1, :], 0.0).then_inc(zeroed, 1)
                pool.wait_ge(zeroed, 2)
                pool.memset(xh[64:65, 1, :], 1.0).then_inc(zeroed, 1)

            @block.tensor
            def _(pe):
                pe.sem_inc(xt_ps, 2)
                with pe.Fori(0, G) as g:
                    pe.wait_ge(xn_done, g * 2 + 1)
                    pe.wait_ge(xt_out, g * 4 + 2)
                    for kt in range(2):
                        for w in range(4):
                            mm = pe.transpose(ptx[0:CK[kt], kt, w * P:(w + 1) * P], xn[:, 0, w, kt * P:kt * P + CK[kt]], ident[:, :])
                    mm.then_inc(xt_ps, 1)
                    pe.wait_ge(xn_done, g * 2 + 2)
                    pe.wait_ge(xt_out, g * 4 + 4)
                    for kt in range(2):
                        mm = pe.transpose(pim[0:CK[kt], kt, 0:P], xn[:, 1, 0, kt * P:kt * P + CK[kt]], ident[:, :])
                    mm.then_inc(xt_ps, 1)
                pe.wait_ge(gready, 1)
                for kt in range(2):
                    mm = pe.matmul(pg[:, 0:E * B], ones[:, :], gp[:, kt, :, :].rearrange("p e b -> p (e b)"), start=(kt == 0), stop=(kt == 1))
                mm.then_inc(gps, 1)

            @block.scalar
            def _(act):
                act.wait_ge(var, 1)
                act.activation(root[:, :], mv[:, :, 1], ACT.Sqrt).then_inc(rooted, 1)
                act.wait_ge(loaded, 80)
                act.activation(w1h[:, :, :, :], w1[:, :, :, :], ACT.Copy).then_inc(w_hi, 1)
                act.activation(w2h[:, :, :, :], w2[:, :, :, :], ACT.Copy).then_inc(w_hi, 1)
                with act.Fori(0, G) as g:
                    for i, (cols, ps) in enumerate(halves):
                        act.wait_ge(xt_ps, g * 2 + i + 3)
                        for kt in range(2):
                            act.activation(cols(xh, kt, g), ps(kt), ACT.Copy).then_inc(xt_hi, 1)
                act.wait_ge(eready, 1)
                act.activation(lg[:, :, :], lg[:, :, :], ACT.Exp).then_inc(edone, 1)

            @block.vector
            def _(v):
                link = chained(v, k.sem("f_chain"))
                v.memset(ones[:, :], 1.0)
                norm_stats(v, Hres, stat, mv4, mv, NTILE // 4, st_sems)
                v.tensor_scalar(mv[:, :, 1], mv[:, :, 1], 1e-5, None, ALU.add).then_inc(var, 1)
                v.wait_ge(rooted, 1)
                newton(v, link, mv[:, :, 1], root[:, :], newt[:, :], rstd[:, :])
                v.sem_inc(xt_out, 4)
                with v.Fori(0, G) as g:
                    v.wait_ge(xt_ps, g * 2 + 2)
                    for w in range(4):
                        ins = v.tensor_scalar(xn[:, 0, w, :], Hres[:, g * 4 + w, :], mv[:, g * 4 + w, 0:1],
                                              rstd[:, ds(g * 4 + w, 1)], ALU.subtract, ALU.mult)
                    ins.then_inc(xn_done, 1)
                    v.tensor_scalar(xn[:, 1, 0, :], Hres[:, g + B, :], mv[:, g + B, 0:1],
                                    rstd[:, ds(g + B, 1)], ALU.subtract, ALU.mult).then_inc(xn_done, 1)
                    for i, (cols, ps) in enumerate(halves):
                        for kt in range(2):
                            v.wait_ge(xt_hi, g * 4 + 2 * i + kt + 1)
                            v.tensor_tensor(cols(xl, kt, g), ps(kt), cols(xh, kt, g), ALU.subtract).then_inc(xt_out, 1)
                v.wait_ge(w_hi, 2)
                for hi, lo, raw in ((w1h, w1l, w1), (w2h, w2l, w2)):
                    v.tensor_tensor(lo[:, :, :, :], raw[:, :, :, :], hi[:, :, :, :], ALU.subtract)
                v.wait_ge(zeroed, 3)
                v.wait_ge(xt_out, 4 + 4 * G)
                for i, x in enumerate((xh, xl)):
                    for kt in range(2):
                        link(v.tensor_reduce(sums[:, i, kt, :], x[:, kt, :].rearrange("p (b n) -> p b n", n=N), AX, ALU.add))
                link(v.tensor_tensor(sumx[:, :, :], sums[:, 0, :, :], sums[:, 1, :, :], ALU.add))
                link(v.tensor_scalar(sumx[:, :, :], sumx[:, :, :], 1.0 / N, None, ALU.mult))
                for kt in range(2):
                    for e in range(E):
                        ins = v.tensor_scalar(gp[:, kt, e, :], sumx[:, kt, :], wg[:, kt, e:e + 1], None, ALU.mult)
                ins.then_inc(gready, 1)
                v.wait_ge(gps, 1)
                link(v.tensor_copy(lg[:, :, :].rearrange("p e b -> p (e b)"), pg[:, 0:E * B]))
                every = lambda a: a[:, :].unsqueeze(1).to_broadcast([P, E, B])
                link(v.tensor_reduce(mx[:, :], lg[:, :, :].rearrange("p e b -> p b e"), AX, ALU.max))
                v.tensor_tensor(lg[:, :, :], lg[:, :, :], every(mx), ALU.subtract).then_inc(eready, 1)
                v.wait_ge(edone, 1)
                link(v.tensor_reduce(tot[:, :], lg[:, :, :].rearrange("p e b -> p b e"), AX, ALU.add))
                link(v.reciprocal(tot[:, :], tot[:, :]))
                link(v.tensor_tensor(lg[:, :, :], lg[:, :, :], every(tot), ALU.mult))
                link(v.tensor_reduce(gw[:, :], lg[:, :, :].rearrange("p e b -> p b e"), AX, ALU.max))
                for e in range(2):
                    link(v.tensor_tensor(hit[:, e, :], lg[:, e, :], gw[:, :], ALU.is_ge))
                    link(v.tensor_scalar(hit[:, e, :], hit[:, e, :], -1.0, 1.0 + e, ALU.mult, ALU.add))
                link(v.tensor_tensor(sel[:, :], hit[:, 0, :], hit[:, 1, :], ALU.mult))
                for j in range(4):
                    r = slice(32 * j, 32 * j + 32)
                    link(v.tensor_copy(gwi[r, :], gw[r, :].rearrange("p (g j) -> p g j", j=4)[:, :, j]))


def newton(v, link, var, root, tmp, rstd):
    link(v.reciprocal(tmp, root))
    link(v.tensor_tensor(tmp, tmp, var, ALU.mult))
    link(v.tensor_tensor(tmp, tmp, root, ALU.add))
    link(v.tensor_scalar(tmp, tmp, 0.5, None, ALU.mult))
    link(v.reciprocal(rstd, tmp))


def experts(k, m):
    out, Hres = k.d["out"], m["H"]
    xh, xl, w1h, w1l, w2h, w2l, sel, gw, gwi, b2 = (m[x] for x in ("xh", "xl", "w1h", "w1l", "w2h", "w2l", "sel", "gw", "gwi", "b2"))
    with ExitStack() as st:
        sb = lambda n, s, t=F32: k.sb(n, s, t, st)
        g, gh, gl = sb("e_g", [P, 2, FT, N]), sb("e_gh", [P, 2, FT, N], BF16), sb("e_gl", [P, 2, FT, N], BF16)
        yb, ot, oi = sb("e_yb", [P, 2, C]), sb("e_ot", [P, 4, C]), sb("e_oi", [P, C])
        yT, b2c, ident = sb("e_yT", [P, 2, P]), m["b2c"], m["ident"]
        p1, p2, p3 = k.ps("e_p1", [P, 2, 2, 512], F32, st), k.ps("e_p2", [P, 2, 512], F32, st), k.ps("e_p3", [P, 512], F32, st)
        h_acc, h_act, g_hi, g_split, y_acc, y_bias, y_out, i_bias, i_rows, i_out, image_out = (
            k.sem("e_" + x) for x in ("h_acc", "h_act", "g_hi", "g_split", "y_acc", "y_bias", "y_out", "i_bias", "i_rows", "i_out", "image_out"))
        g_room, passed = k.sem("e_g_room"), k.sem("e_passed")
        sent = [k.sem(f"e_sent{j}") for j in range(4)]

        def steps(eng, body):
            for kk in range(4):
                body(0, kk)
            with eng.Fori(1, G) as i:
                for kk in range(4):
                    body(i, kk)
            for kk in range(2):
                body(G, kk)

        def batch(c, kk, lag):
            kk -= lag
            if isinstance(c, int) and not 0 <= c * 4 + kk < B:
                return None
            return c * 4 + kk, kk % 4, kk % 2, c + kk // 4

        with k.nc.Block() as block:
            @block.sync
            def _(sp):
                def body(c, kk):
                    y = batch(c, kk, 0)
                    if y is not None:
                        n, j, u, grp = y
                        wait_apart(sp, y_out, n + 2, passed)
                        sp.dma_start(out[n, NI:N, :], ot[:, j, :]).then_inc(sent[j], 16)
                        if j == 3:
                            wait_apart(sp, i_out, grp + 2, passed)
                            for q in range(4):
                                sp.dma_start(out[grp * 4 + q, 0:NI, :], oi[32 * q + ID:32 * q + 32, :]).then_inc(image_out, 16)
                with sp.Fori(0, G) as i:
                    for kk in range(4):
                        body(i, kk)
                for q in range(4):
                    sp.wait_ge(sent[q], 16 * G + 16)
                sp.wait_ge(image_out, 64 * G + 64)

            @block.tensor
            def _(pe):
                def body(c, kk):
                    y = batch(c, kk, 0)
                    if y is not None:
                        n, j, u, grp = y
                        e = pe.value_load(sel[0:1, ds(n, 1)], min_val=0, max_val=E - 1)
                        pe.wait_ge(h_act, n * 2 + 2)
                        for f in range(FT):
                            o = p1[:, u, f // 3, (f % 3) * N:(f % 3 + 1) * N]
                            fs = slice(f * P, (f + 1) * P)
                            parts = [(w, x, kt) for w, x in ((w1h, xh), (w1l, xh), (w1h, xl)) for kt in range(2)]
                            for a, (w, x, kt) in enumerate(parts):
                                mm = pe.matmul(o, w[:, kt, e, fs], x[:, kt, ds(n * N, N)], start=(a == 0), stop=(a == 5))
                            if f % 3 == 2:
                                mm.then_inc(h_acc, 1)
                    y = batch(c, kk, 2)
                    if y is not None and y[1] == 3:
                        grp = y[3]
                        pe.wait_ge(i_bias, grp * 4 + 4)
                        pe.wait_ge(i_out, grp + 1)
                        for kt in range(2):
                            mm = pe.transpose(p3[:, kt * P:kt * P + CK[kt]], yT[0:CK[kt], kt, :], ident[0:CK[kt], 0:CK[kt]])
                        mm.then_inc(i_rows, 1)
                    y = batch(c, kk, 1)
                    if y is not None:
                        n, j, u, grp = y
                        e = pe.value_load(sel[0:1, ds(n, 1)], min_val=0, max_val=E - 1)
                        pe.wait_ge(g_split, n + 1)
                        pe.wait_ge(y_bias, n + 1)
                        parts = [(a, w, f) for f in range(FT) for a, w in ((gh, w2h), (gh, w2l), (gl, w2h))]
                        for b, (a, w, f) in enumerate(parts):
                            pe.matmul(p2[:, u, 0:C], a[:, u, f, 0:NT], w[:, e, f, :], start=(b == 0), stop=(b == 3 * FT - 1))
                        for kt in range(2):
                            for b, (a, w, f) in enumerate(parts):
                                mm = pe.matmul(p2[0:CK[kt], u, C + 32 * kt:C + 32 * kt + 32], w[:, e, f, kt * P:kt * P + CK[kt]], a[:, u, f, IW:N],
                                               start=(b == 0), stop=(b == 3 * FT - 1))
                        mm.then_inc(y_acc, 1)
                steps(pe, body)

            @block.scalar
            def _(act):
                act.sem_inc(h_act, 4)
                with act.Fori(0, B // 2) as i:
                    for u in range(2):
                        n = i * 2 + u
                        act.wait_ge(g_room, n + 1)
                        for b in range(2):
                            act.wait_ge(h_acc, n * 2 + b + 1)
                            act.activation(g[:, u, 3 * b:3 * b + 3, :].rearrange("p f n -> p (f n)"), p1[:, u, b, 0:3 * N], ACT.Gelu).then_inc(h_act, 1)

            @block.vector
            def _(v):
                v.sem_inc(g_room, 2)
                v.sem_inc(y_bias, 2)
                v.sem_inc(i_out, 1)
                v.sem_inc(i_rows, 1)
                v.sem_inc(y_out, 1)
                v.sem_inc(image_out, 64)
                for q in range(4):
                    v.sem_inc(sent[q], 16)

                def body(c, kk):
                    y = batch(c, kk, 0)
                    if y is not None:
                        n, j, u, grp = y
                        v.wait_ge(h_act, n * 2 + 6)
                        if not (isinstance(c, int) and n < 2):
                            v.wait_ge(y_acc, n - 1)
                        v.tensor_copy(gh[:, u, :, :], g[:, u, :, :]).then_inc(g_hi, 1)
                        v.wait_ge(g_hi, n + 1)
                        v.tensor_tensor(gl[:, u, :, :], g[:, u, :, :], gh[:, u, :, :], ALU.subtract).then_inc(g_split, 1)
                        v.wait_ge(g_split, n + 1)
                        v.sem_inc(g_room, 1)
                    y = batch(c, kk, 1)
                    if y is not None:
                        n, j, u, grp = y
                        e = v.value_load(sel[0:1, ds(n, 1)], min_val=0, max_val=E - 1)
                        v.wait_ge(y_acc, n + 1)
                        v.wait_ge(y_out, n + 1)
                        v.tensor_tensor(yb[:, u, :], p2[:, u, 0:C], b2[:, e, :], ALU.add).then_inc(y_bias, 1)
                        v.wait_ge(i_rows, grp + 1)
                        for kt in range(2):
                            ins = v.tensor_scalar(yT[0:CK[kt], kt, 32 * j:32 * j + 32], p2[0:CK[kt], u, C + 32 * kt:C + 32 * kt + 32],
                                                  b2c[0:CK[kt], kt, ds(e, 1)], None, ALU.add)
                        ins.then_inc(i_bias, 1)
                        v.wait_ge(y_bias, n + 3)
                        v.wait_ge(sent[j], grp * 16 + 16)
                        v.scalar_tensor_tensor(ot[:, j, :], yb[:, u, :], gw[:, ds(n, 1)], Hres[:, n, :], ALU.mult, ALU.add).then_inc(y_out, 1)
                    y = batch(c, kk, 2)
                    if y is not None and y[1] == 3:
                        grp = y[3]
                        v.wait_ge(i_rows, grp + 2)
                        v.wait_ge(image_out, grp * 64 + 64)
                        v.scalar_tensor_tensor(oi[:, :], p3[:, 0:C], gwi[:, ds(grp, 1)], Hres[:, B + grp, :], ALU.mult, ALU.add).then_inc(i_out, 1)
                steps(v, body)


def build(nc, d):
    with ExitStack() as stack:
        k = Ctx(nc, stack, d)
        m = {}
        m["H"] = k.sb("Hres", [P, NTILE, C])
        m["ident"] = k.sb("ident", [P, P])
        m["identb"] = k.sb("identb", [P, P], BF16)
        m["qx"], m["qh"], m["qa"], m["qo"], m["qp"] = (k.sb(x, [P, 4]) for x in ("qx", "qh", "qa", "qo", "qp"))
        m["ap"], m["ad"], m["biasp"], m["biasd"] = k.sb("ap", [P, 9]), k.sb("ad", [P, 5]), k.sb("biasp", [P, 9]), k.sb("biasd", [P, 5])
        att = ExitStack()
        m["con"] = k.sb("con", [P, 8])
        m["qkflat"] = k.sb("qk", [P, 6 * T], BF16, att)[:, :]
        m["qk"] = m["qkflat"].rearrange("p (b t n) -> p b t n", b=B, n=N)
        att2 = ExitStack()
        m["rmax"] = k.sb("rmax", [P, B, RT], F32, att2)
        m["vt"], m["vi"] = k.sb("vt", [P, B, 3 * P], BF16, att2), k.sb("vi", [P, G, 3 * P], BF16, att2)
        mid = ExitStack()
        with mid:
            m["xqT"], m["wqT"] = k.sb("xqT", [P, 2, T], BF16, mid), k.sb("wqT", [P, 2, 9 * P], BF16, mid)
            m["xqI"] = k.sb("xqI", [P, 2, G * P], BF16, mid)
            m["wdT"] = k.sb("wdT", [P, 2, 5 * P], BF16, mid)
            m["xnT"] = m["qkflat"][:, 0:4 * T].bitcast(F32).rearrange("p (t n) -> p t n", t=2)
            embed(k, m)
            quant_inputs(k, m)
            range_h(k, m)
            quant_qkv(k, m)
        with att:
            m["vbd"] = k.sb("vbd", [P, B, HT, 4, 32], BF16, att2)
            range_scores(k, m)
            attention(k, m)
            att2.close()
            project(k, m)
        m["xh"], m["xl"] = k.sb("xh", [P, 2, T], BF16), k.sb("xl", [P, 2, T], BF16)
        m["w1h"], m["w1l"] = k.sb("w1h", [P, 2, E, FF], BF16), k.sb("w1l", [P, 2, E, FF], BF16)
        m["w2h"], m["w2l"] = k.sb("w2h", [P, E, FT, C], BF16), k.sb("w2l", [P, E, FT, C], BF16)
        m["sel"], m["gw"], m["gwi"], m["b2"], m["b2c"] = k.sb("sel", [P, B], I32), k.sb("gw", [P, B]), k.sb("gwi", [P, G]), k.sb("b2", [P, E, C]), k.sb("b2c", [P, 2, E])
        ffn_inputs(k, m)
        experts(k, m)


def layout(i):
    f = {n: np.ascontiguousarray(np.asarray(a)) for n, a in i.items()}
    r = {}
    x = f["x"][:, :, :80, :80].reshape(B, 3, 5, 16, 5, 16).transpose(1, 3, 5, 0, 2, 4).reshape(768, B, NI)
    xp = np.zeros((768, B, 32), np.float32)
    xp[:, :, 32 - NI:] = x
    r["patches"] = xp.reshape(KI, P, G * P).transpose(1, 0, 2)
    r["wimg"] = f["L0_tok_conv_w"].reshape(C, 768).T.reshape(KI, P, C).transpose(1, 0, 2)
    side = np.searchsorted(np.arange(1 / 32, 1.0, 1 / 32, dtype=np.float32), np.arange(0.0, 1.0 - 1e-6, 0.2, dtype=np.float32), side="right")
    pos = np.zeros((32, C), np.float32)
    pos[32 - NI:] = f["L0_tok_pos_table"][(side[:, None] * 32 + side).reshape(-1)]
    r["posimg"] = np.tile(pos, (4, 1))
    rows = lambda a: np.broadcast_to(a, (P, a.shape[-1]))
    r["convb"], r["gamma"], r["beta"] = rows(f["L0_tok_conv_b"]), rows(f["L0_txt_ln_gamma"]), rows(f["L0_txt_ln_beta"])
    r["postxt"] = f["L0_txt_pos_table"][:NT]
    cf = np.zeros((P, C), np.float32)
    cf[0:40] = cf[64:104] = f["L0_txt_poly_coeffs"].transpose(1, 0, 2).reshape(40, C)
    r["coef"] = cf
    r["ids"] = f["x_txt"].T
    r["turns"] = f["L0_txt_turns"]
    qw, qb = f["L0_attn_qkv_w"], f["L0_attn_qkv_b"]
    wc = np.zeros((2 * P, 3 * C), np.float32)
    wc[:C] = qw.T
    r["wc"] = wc.reshape(2, P, 3 * C).transpose(1, 0, 2)
    wp, bp = np.zeros((3 * H, 32, C), np.float32), np.zeros((3 * H, 32), np.float32)
    wp[:, :HD], bp[:, :HD] = qw.reshape(3 * H, HD, C), qb.reshape(3 * H, HD)
    r["wp"], r["biasp"] = wp.reshape(9, P, C).transpose(1, 0, 2), bp.reshape(9, P).T
    dense = [slice(i, i + P) for i in (0, 128, 256, 384, 448)]
    r["wd"], r["biasd"] = np.stack([qw[i] for i in dense], 1), np.stack([qb[i] for i in dense], 1)
    pwr = np.zeros((2 * P, H, 32), np.float32)
    pwr[:C, :, :HD] = f["L0_attn_proj_w"].reshape(C, H, HD)
    r["wproj"] = pwr.reshape(2, P, H * 32).transpose(1, 0, 2)
    r["projb"] = rows(f["L0_attn_proj_b"])
    r["pad"] = np.repeat(np.where(np.arange(P) % 32 < HD, BIG, -BIG).astype(np.float32)[:, None], 2, 1)
    w1 = np.zeros((2 * P, E, FF), np.float32)
    w1[:C], w1[C] = f["L0_ffn_W1"].transpose(1, 0, 2), f["L0_ffn_b1"]
    r["w1"] = w1.reshape(2, P, E, FF).transpose(1, 0, 2, 3)
    r["w2"] = f["L0_ffn_W2"].reshape(E, FT, P, C).transpose(2, 0, 1, 3)
    wg = np.zeros((2 * P, E), np.float32)
    wg[:C] = f["L0_ffn_Wg"].T
    r["wg"] = wg.reshape(2, P, E).transpose(1, 0, 2)
    b2 = np.zeros((2 * P, E), np.float32)
    b2[:C] = f["L0_ffn_b2"].T
    r["b2c"] = b2.reshape(2, P, E).transpose(1, 0, 2)
    r["b2"] = np.broadcast_to(f["L0_ffn_b2"], (P, E, C))
    return {n: np.ascontiguousarray(a) for n, a in r.items()}


def kernel(**inputs):
    from concourse import bacc
    from concourse.bass_utils import run_bass_kernel_spmd
    arrays = layout(inputs)
    nc = bacc.Bacc("TRN2", target_bir_lowering=False, num_devices=1)
    d = {n: nc.dram_tensor("in_" + n, a.shape, mybir.dt.from_np(a.dtype), kind="ExternalInput").ap() for n, a in arrays.items()}
    d["out"] = nc.dram_tensor("out_0", (B, N, C), F32, kind="ExternalOutput").ap()
    build(nc, d)
    nc.compile()
    res = run_bass_kernel_spmd(nc, [{"in_" + n: a for n, a in arrays.items()}], core_ids=[0])
    return res.results[0]["out_0"]
```
